# Optimizing a Trainium2 kernel written in Bass

```python
import numpy as np
import jax
import jax.numpy as jnp

def _softmax(x, axis=-1):
    return jax.nn.softmax(x, axis=axis)

def _gelu(x):
    return jax.nn.gelu(x, approximate=True)

def _silu(x):
    return jax.nn.silu(x)

def _sigmoid(x):
    return jax.nn.sigmoid(x)

def _layernorm(x, axis=-1, eps=1e-05):
    m = jnp.mean(x, axis=axis, keepdims=True)
    v = jnp.var(x, axis=axis, keepdims=True)
    return (x - m) / jnp.sqrt(v + eps)

def _scatter_add(tgt, idx, src, axis=0):
    return tgt.at[idx].add(src)

def _segment_sum(src, seg, n):
    return jax.ops.segment_sum(src, seg, n)
kernel_name = 'mk_xattn_ffn_d1_seqx_r4_17b2b6'

def setup_inputs(seed: int=0):
    np.random.seed(seed)
    _w = jnp.asarray

    def _rec_inputs():
        import jax
        import jax.numpy as jnp
        _rk = jax.random.key(seed)
        x = 7.22e-05 + 1 * jax.random.normal(jax.random.fold_in(_rk, 1), (1, 2048, 256), jnp.float32)
        _lenS = 2048 - jax.random.randint(jax.random.fold_in(_rk, 7), (1,), 0, max(1, 2048 // 4) + 1, jnp.int32)
        _lenS2 = 1601 - jax.random.randint(jax.random.fold_in(_rk, 8), (1,), 0, max(1, 1601 // 4) + 1, jnp.int32)
        _ctx_1024P = jax.random.normal(jax.random.fold_in(_rk, 11), (1, 16, 256), jnp.float32)
        _ctx_1024c = jax.random.dirichlet(jax.random.fold_in(_rk, 511), 0.3 * jnp.ones((16,), jnp.float32), (1, 1601))
        _ctx_1024t = jnp.einsum('bsk,bkd->bsd', _ctx_1024c, _ctx_1024P)
        _ctx_1024t = _ctx_1024t * jax.lax.rsqrt(jnp.mean(jnp.square(_ctx_1024t)) + 1e-12) * 0.953939
        ctx_1024 = 4.13588e-05 + 0.999923 * (_ctx_1024t + 0.3 * jax.random.normal(jax.random.fold_in(_rk, 611), (1, 1601, 256), jnp.float32))
        return (x, ctx_1024)
    x, ctx_1024 = _rec_inputs()

    def _L0_xattn_setup():
        import jax, jax.numpy as jnp
        import numpy as np
        B, S, D, DFF = (4, 512, 256, 1024)
        EPS = 1e-05

        def layernorm(x, gamma, beta):
            mu = jnp.mean(x, axis=-1, keepdims=True)
            var = jnp.var(x, axis=-1, keepdims=True)
            return (x - mu) * jax.lax.rsqrt(var + EPS) * gamma + beta

        def attention(Q, K, V, causal):
            d_k = Q.shape[-1]
            scores = jnp.einsum('bqd,bkd->bqk', Q, K) / jnp.sqrt(jnp.asarray(d_k, Q.dtype))
            if causal:
                q_len, k_len = (scores.shape[-2], scores.shape[-1])
                mask = jnp.tril(jnp.ones((q_len, k_len), dtype=bool))
                scores = jnp.where(mask[None], scores, jnp.asarray(-jnp.inf, scores.dtype))
            w = jax.nn.softmax(scores, axis=-1)
            return jnp.einsum('bqk,bkd->bqd', w, V)
        key = jax.random.key(seed)
        ks = jax.random.split(key, 12)
        sd = 0.02
        return {'y': jax.random.normal(ks[0], (B, S, D), jnp.float32), 'Z': jax.random.normal(ks[1], (B, S, D), jnp.float32), 'w1': jax.random.normal(ks[2], (D, DFF), jnp.float32) * sd, 'b1': jnp.zeros((DFF,), jnp.float32), 'w2': jax.random.normal(ks[3], (DFF, D), jnp.float32) * sd, 'b2': jnp.zeros((D,), jnp.float32), 'g1': jnp.ones((D,), jnp.float32), 'beta1': jnp.zeros((D,), jnp.float32), 'g2': jnp.ones((D,), jnp.float32), 'beta2': jnp.zeros((D,), jnp.float32), 'g3': jnp.ones((D,), jnp.float32), 'beta3': jnp.zeros((D,), jnp.float32)}
    _L0_xattn_all = _L0_xattn_setup()
    _L0_xattn_in = {k: v for k, v in _L0_xattn_all.items() if k in ('w1', 'b1', 'w2', 'b2', 'g1', 'beta1', 'g2', 'beta2', 'g3', 'beta3')}
    del _L0_xattn_all

    def _L0_ffn_setup():
        import jax, jax.numpy as jnp
        import numpy as np
        TOP_K = 2
        key = jax.random.key(seed)
        k0, k1, k2, k3, k4 = jax.random.split(key, 5)
        B, S, H, I, E = (1, 1024, 256, 512, 8)
        hidden_states = jax.random.normal(k0, (B, S, H), dtype=jnp.float32)
        wg = jax.random.normal(k1, (E, H), dtype=jnp.float32) * 0.02
        w1 = jax.random.normal(k2, (E, I, H), dtype=jnp.float32) * 0.02
        w3 = jax.random.normal(k3, (E, I, H), dtype=jnp.float32) * 0.02
        w2 = jax.random.normal(k4, (E, H, I), dtype=jnp.float32) * 0.02
        return {'hidden_states': hidden_states, 'wg': wg, 'w1': w1, 'w3': w3, 'w2': w2}
    _L0_ffn_all = _L0_ffn_setup()
    _L0_ffn_in = {k: v for k, v in _L0_ffn_all.items() if k in ('wg', 'w1', 'w3', 'w2')}
    del _L0_ffn_all
    return {'x': x, 'ctx_1024': ctx_1024, 'L0_xattn_w1': _L0_xattn_in['w1'], 'L0_xattn_b1': _L0_xattn_in['b1'], 'L0_xattn_w2': _L0_xattn_in['w2'], 'L0_xattn_b2': _L0_xattn_in['b2'], 'L0_xattn_g1': _L0_xattn_in['g1'], 'L0_xattn_beta1': _L0_xattn_in['beta1'], 'L0_xattn_g2': _L0_xattn_in['g2'], 'L0_xattn_beta2': _L0_xattn_in['beta2'], 'L0_xattn_g3': _L0_xattn_in['g3'], 'L0_xattn_beta3': _L0_xattn_in['beta3'], 'L0_ffn_wg': _L0_ffn_in['wg'], 'L0_ffn_w1': _L0_ffn_in['w1'], 'L0_ffn_w3': _L0_ffn_in['w3'], 'L0_ffn_w2': _L0_ffn_in['w2']}

def reference(x, ctx_1024, L0_xattn_w1, L0_xattn_b1, L0_xattn_w2, L0_xattn_b2, L0_xattn_g1, L0_xattn_beta1, L0_xattn_g2, L0_xattn_beta2, L0_xattn_g3, L0_xattn_beta3, L0_ffn_wg, L0_ffn_w1, L0_ffn_w3, L0_ffn_w2):
    import jax
    import jax.numpy as jnp

    def _L0_xattn_ref(y, Z, w1, b1, w2, b2, g1, beta1, g2, beta2, g3, beta3):
        import jax, jax.numpy as jnp
        import numpy as np
        B, S, D, DFF = (4, 512, 256, 1024)
        EPS = 1e-05

        def layernorm(x, gamma, beta):
            mu = jnp.mean(x, axis=-1, keepdims=True)
            var = jnp.var(x, axis=-1, keepdims=True)
            return (x - mu) * jax.lax.rsqrt(var + EPS) * gamma + beta

        def attention(Q, K, V, causal):
            d_k = Q.shape[-1]
            scores = jnp.einsum('bqd,bkd->bqk', Q, K) / jnp.sqrt(jnp.asarray(d_k, Q.dtype))
            if causal:
                q_len, k_len = (scores.shape[-2], scores.shape[-1])
                mask = jnp.tril(jnp.ones((q_len, k_len), dtype=bool))
                scores = jnp.where(mask[None], scores, jnp.asarray(-jnp.inf, scores.dtype))
            w = jax.nn.softmax(scores, axis=-1)
            return jnp.einsum('bqk,bkd->bqd', w, V)
        sa = attention(y, y, y, causal=True)
        y = layernorm(y + sa, g1, beta1)
        ca = attention(y, Z, Z, causal=False)
        y = layernorm(y + ca, g2, beta2)
        h = jax.nn.relu(jnp.einsum('bsd,df->bsf', y, w1) + b1)
        ff = jnp.einsum('bsf,fd->bsd', h, w2) + b2
        y = layernorm(y + ff, g3, beta3)
        return y

    def _L0_ffn_ref(hidden_states, wg, w1, w3, w2):
        import jax, jax.numpy as jnp
        import numpy as np
        TOP_K = 2
        orig_shape = hidden_states.shape
        H = orig_shape[-1]
        E = wg.shape[0]
        x = hidden_states.reshape(-1, H)
        router_logits = x @ wg.T
        probs = jax.nn.softmax(router_logits, axis=-1)
        topk_w, topk_idx = jax.lax.top_k(probs, TOP_K)
        topk_w = topk_w / jnp.sum(topk_w, axis=-1, keepdims=True)
        expert_w = jnp.sum(jax.nn.one_hot(topk_idx, E, dtype=x.dtype) * topk_w[..., None], axis=1)
        h1 = jnp.einsum('th,eih->tei', x, w1)
        h3 = jnp.einsum('th,eih->tei', x, w3)
        y = jnp.einsum('tei,ehi->teh', jax.nn.silu(h1) * h3, w2)
        out = jnp.einsum('te,teh->th', expert_w, y)
        return out.reshape(orig_shape)
    x = x + _L0_xattn_ref(_layernorm(x, axis=-1), ctx_1024, L0_xattn_w1, L0_xattn_b1, L0_xattn_w2, L0_xattn_b2, L0_xattn_g1, L0_xattn_beta1, L0_xattn_g2, L0_xattn_beta2, L0_xattn_g3, L0_xattn_beta3)
    x = x + _L0_ffn_ref(_layernorm(x, axis=-1), L0_ffn_wg, L0_ffn_w1, L0_ffn_w3, L0_ffn_w2)
    return x

_drawn_inputs = setup_inputs


def setup_inputs(seed=0):
    import zlib

    import numpy as np

    out = dict(_drawn_inputs(seed))
    spreads = {'L0_xattn_b1': (0.0, 0.362),
     'L0_xattn_b2': (0.0, 0.1),
     'L0_xattn_g1': (1.0, 0.2),
     'L0_xattn_beta1': (0.0, 0.1),
     'L0_xattn_g2': (1.0, 0.2),
     'L0_xattn_beta2': (0.0, 0.1),
     'L0_xattn_g3': (1.0, 0.2),
     'L0_xattn_beta3': (0.0, 0.1)}
    factors = {'L0_ffn_wg': 7.48, 'L0_ffn_w1': 6.58, 'L0_ffn_w3': 6.507, 'L0_ffn_w2': 6.51}
    for name, (base, spread) in spreads.items():
        noise = np.random.default_rng([zlib.crc32(name.encode()), seed]).standard_normal(out[name].shape)
        drawn = base * np.exp(spread * noise) if base else spread * noise
        out[name] = jnp.asarray(drawn.astype(out[name].dtype))
    for name, factor in factors.items():
        out[name] = (out[name] * factor).astype(out[name].dtype)
    return out
```

```python
import numpy as np
import concourse.bass as bass
from concourse import mybir
from contextlib import ExitStack

F32, F16, U32, I32 = mybir.dt.float32, mybir.dt.float16, mybir.dt.uint32, mybir.dt.int32
ALU = mybir.AluOpType
ACT = mybir.ActivationFunctionType
X = mybir.AxisListType.X

P = 128
S, D = 2048, 256
L = 1601
DFF = 1024
NE, NI = 8, 512
NT = S // P
KD = D // P
NZ = -(-L // P)
ZR = L - (NZ - 1) * P
KF = DFF // P
KI = NI // P
CH = 4 * P
TB = 4
NB = NT // TB
EPS = 1e-5
WS = 64.0
SM = float(D) ** -0.5
MASKED = -60000.0
EW = KD * 2 * NI + KI * D

PARTS = ((0, 0), (0, 1), (1, 0))


def xattn_ffn_moe(nc, x, z, zT, w1, w2, wgT, we, b1, rows, out):
    with ExitStack() as ctx:
        def sb(name, shape, dt=F32):
            return ctx.enter_context(nc.sbuf_tensor(name, shape, dt))

        def sem(name):
            return ctx.enter_context(nc.semaphore(name))

        ident = sb("ident", [P, P])
        ident16 = sb("ident16", [P, P], F16)
        mask = sb("mask", [P, P], F16)
        expo = sb("expo", [P, 1])
        bridge = sb("bridge", [P, 2])
        iota8 = sb("iota8", [P, NE])
        vec = sb("vec", [P, 7, D])
        b1c = sb("b1c", [P, KF])
        w1s = sb("w1s", [P, 2, KD, DFF], F16)
        w2s = sb("w2s", [P, 2, KF, D], F16)
        wgs = sb("wgs", [P, 2, KD, NE], F16)
        wgf = sb("wgf", [P, KD, NE])
        y = sb("y", [P, NT, D])
        xin = sb("xin", [P, 2, D])
        yT = sb("yT", [P, 2, KD, NT, P], F16)
        yv = sb("yv", [P, 2, NT, D], F16)
        zs = sb("zs", [P, 2, NZ, D], F16)
        zTs = sb("zTs", [P, 2, KD, L], F16)
        stage = sb("stage", [P, EW])
        prob = sb("prob", [P, 2, NT * P])
        probT = sb("probT", [P, 2, 2, NT, P], F16)
        qst = sb("qst", [P, 2, D])
        qT = sb("qT", [P, 2, 2, KD, P], F16)
        yst = sb("yst", [P, TB, D])
        ybT = sb("ybT", [P, 2, KD, CH], F16)
        hid = sb("hid", [P, 2, CH])
        hidT = sb("hidT", [P, 2, KF, CH], F16)
        cmax = sb("cmax", [P, 2, 4])
        nmax = sb("nmax", [P, 2, 1])
        nbias = sb("nbias", [P, 2, 1])
        esum = sb("esum", [P, 2, 4])
        rsum = sb("rsum", [P, 2, 1])
        rinv = sb("rinv", [P, 2, 1])
        u = sb("u", [P, 2, D])
        stat = sb("stat", [P, 2, 6])
        mv = sb("mv", [P, 2, 2])
        veps = sb("veps", [P, 2, 1])
        rstd = sb("rstd", [P, 2, 1])
        nrm = sb("nrm", [P, 2, D])
        gam = sb("gam", [P, 2, D])
        lg = sb("lg", [P, 2, NE])
        top = sb("top", [P, 2, 8])
        topi = sb("topi", [P, 2, 8], U32)
        topf = sb("topf", [P, 2, 2])
        dl = sb("dl", [P, 2, 1])
        gt = sb("gt", [P, 2, 4])
        oh = sb("oh", [P, 2, 2, NE])
        gate = sb("gate", [P, NT, NE])
        ew = sb("ew", [P, 2, 2, EW], F16)
        sil = prob[:, 0, :2 * NI].rearrange("p (q n) -> p q n", q=2)
        act = prob[:, 1, :2 * NI].rearrange("p (q n) -> p q n", q=2)
        actT = probT[:, 0, :, :2 * KI, :].rearrange("p a (q k) t -> p q a k t", q=2)

        ps = [ctx.enter_context(nc.psum_tensor(f"ps{n}", [P, CH], F32)) for n in range(8)]
        psT = ps[4:6]
        psO = ps[6:8]

        names = """vec_in b1_in x_in0 x_in1 consts stage_in stage_scaled stage_hi stage_lo
            l0_stat l0_agg l0_var l0_rstd l0_nrm l0_copy l0_vhi l0_vlo l0_tr l0_hi l0_lo
            s_scores s_cmax s_nmax s_bias s_exp s_tr s_hi s_lo s_pv s_rsum s_rinv s_u s_stat s_agg s_var
            s_rstd s_nrm s_gam s_y
            c_scores c_cmax c_nmax c_bias c_exp c_tr c_hi c_lo c_pv c_rsum c_rinv c_u c_stat c_agg c_var
            c_rstd c_nrm c_gam c_y c_qst c_qtr c_qhi c_qlo
            f_yst f_ytr f_yhi f_ylo f_up f_relu f_hi f_lo f_down
            n_yb n_u n_stat n_agg n_var n_rstd n_nrm n_gam n_y3 x2_in0 x2_in1 x1_done
            m_stat m_agg m_var m_rstd m_nrm h_tr h_hi h_lo r_logit r_lg r_top r_topi r_topf r_dl r_exp r_den
            r_w1 r_w2 r_oh r_g1 r_gate
            e_in e_scaled e_hi e_lo e_up e_sil e_act e_tr e_ahi e_alo e_down e_acc out_done""".split()
        sm = {n: sem(n) for n in names}

        NST = 3 + 7
        zmain = (NZ - 1) * P

        def stv(a, n):
            return stage[:, :a * n].rearrange("p (a n) -> p a n", a=a)

        chunks = []
        for j in range(2):
            n = (NZ - 1) // 2
            chunks.append((z[j * n * P:(j + 1) * n * P, :].rearrange("(a p) d -> p a d", p=P), stv(n, D),
                           zs[:, :, j * n:(j + 1) * n, :], 1.0, P))
        chunks.append((z[zmain:L, :], stage[:ZR, :D], zs[:ZR, :, NZ - 1, :], 1.0, ZR))
        for k in range(KD):
            chunks.append((zT[k * P:(k + 1) * P, :], stage[:, :L], zTs[:, :, k, :], 1.0, P))
        chunks.append((w1.rearrange("(k p) f -> p k f", p=P), stv(KD, DFF), w1s, WS, P))
        chunks.append((w2.rearrange("(k p) d -> p k d", p=P), stv(KF, D), w2s, WS, P))
        chunks.append((wgT.rearrange("(k p) e -> p k e", p=P), stv(KD, NE), wgs, WS, P))
        NC = len(chunks)

        def part(t, n):
            return t[:, n]

        def wait(eng, name, n):
            eng.wait_ge(sm[name], n)

        def bridge_dve():
            nc.vector.memset(bridge[:, 0:1], 0.0)

        def bridge_pool():
            nc.gpsimd.tensor_tensor(bridge[:, 1:2], expo[:], expo[:], ALU.mult)

        def chunk_of(i):
            return -(-(i + 1) // 4)

        S_CH = [0]
        for i in range(NT):
            S_CH.append(S_CH[-1] + chunk_of(i))
        C_CH = -(-L // CH)
        CW = [CH] * (C_CH - 1) + [L - CH * (C_CH - 1)]

        block = ctx.enter_context(nc.Block())

        @block.sync
        def _(sp):
            sp.dma_start(vec[:].rearrange("p a d -> p (a d)"), rows.partition_broadcast(P)).then_inc(sm["vec_in"], 16)
            sp.dma_start(b1c[:], b1).then_inc(sm["b1_in"], 16)
            def load_x(t, q, name):
                sp.dma_start(xin[:, q, :], x[bass.ds(t * P, P), :]).then_inc(sm[name + str(q)], 16)

            for q in range(2):
                load_x(q, q, "x_in")
            with sp.Fori(2, NT - 1, 2) as i:
                for q in range(2):
                    sp.wait_ge(sm["l0_nrm"], i + (q - 1))
                    load_x(i + q, q, "x_in")
            for n, (src, dst, _, _, _) in enumerate(chunks):
                if n:
                    wait(sp, "stage_lo", n)
                sp.dma_start(dst, src).then_inc(sm["stage_in"], 16)
            wait(sp, "l0_nrm", NT)
            for q in range(2):
                load_x(q, q, "x2_in")
            with sp.Fori(2, NT - 1, 2) as i:
                for q in range(2):
                    sp.wait_ge(sm["x1_done"], i + q)
                    load_x(i + q, q, "x2_in")
            for e in range(NE):
                if e == 0:
                    wait(sp, "stage_lo", NC)
                else:
                    wait(sp, "e_lo", e)
                sp.dma_start(stage[:], we[e]).then_inc(sm["e_in"], 16)
            with sp.Fori(0, NT) as i:
                sp.wait_ge(sm["e_acc"], i + (NE - 1) * NT + 1)
                sp.dma_start(out[bass.ds(i * P, P), :], y[:, i, :]).then_inc(sm["out_done"], 16)
            wait(sp, "out_done", 16 * NT)

        @block.gpsimd
        def _(pool):
            g = nc.gpsimd
            g.memset(ident[:], 0.0).then_inc(sm["consts"], 1)
            g.memset(ident16[:], 0.0).then_inc(sm["consts"], 1)
            g.memset(mask[:], 0.0).then_inc(sm["consts"], 1)
            g.memset(expo[:], -0.5).then_inc(sm["consts"], 1)
            g.iota(iota8[:], pattern=[[1, NE]], base=0, channel_multiplier=0,
                   allow_small_or_imprecise_dtypes=True).then_inc(sm["consts"], 1)
            g.memset(y[:, 0, 0:1], 0.0).then_inc(sm["x1_done"], 1)
            wait(pool, "consts", 5)
            for t in (ident, ident16):
                g.affine_select(out=t[:], in_=t[:], compare_op=ALU.not_equal, fill=1.0, base=0,
                                pattern=[[-1, P]], channel_multiplier=1).then_inc(sm["consts"], 1)
            g.affine_select(out=mask[:], in_=mask[:], compare_op=ALU.is_ge, fill=MASKED, base=0,
                            pattern=[[-1, P]], channel_multiplier=1).then_inc(sm["consts"], 1)
            with pool.Fori(0, NT - 1, 2) as i:
                for q in range(2):
                    t = i + q
                    pool.wait_ge(sm["l0_var"], t + 1)
                    g.tensor_tensor(rstd[:, q, :], veps[:, q, :], expo[:], ALU.pow).then_inc(sm["l0_rstd"], 1)
                    pool.wait_ge(sm["l0_nrm"], t + 1)
                    g.tensor_copy(y[:, t, :], nrm[:, q, :]).then_inc(sm["l0_copy"], 1)
                    pool.wait_ge(sm["l0_vhi"], t + 1)
                    bridge_pool()
                    g.tensor_tensor(yv[:, 1, t, :], nrm[:, q, :], yv[:, 0, t, :], ALU.subtract).then_inc(sm["l0_vlo"], 1)

            def stage_scale(n):
                _, src, _, scale, _ = chunks[n]
                wait(pool, "stage_in", 16 * (n + 1))
                g.tensor_scalar(src, src, scale, None, ALU.mult).then_inc(sm["stage_scaled"], 1)

            def stage_lo(n):
                _, src, dst, _, rows_ = chunks[n]
                wait(pool, "stage_hi", n + 1)
                hi, lo = (dst[:, 0], dst[:, 1])
                g.tensor_tensor(lo, src, hi, ALU.subtract).then_inc(sm["stage_lo"], 1)

            def ln_rstd(pre, i, q):
                pool.wait_ge(sm[pre + "var"], i + 1)
                g.tensor_tensor(rstd[:, q, :], veps[:, q, :], expo[:], ALU.pow).then_inc(sm[pre + "rstd"], 1)

            def ln_affine(pre, i, q, row):
                pool.wait_ge(sm[pre + "nrm"], i + 1)
                g.tensor_tensor(gam[:, q, :], nrm[:, q, :], vec[:, row, :], ALU.mult).then_inc(sm[pre + "gam"], 1)
                pool.wait_ge(sm[pre + "gam"], i + 1)
                bridge_pool()
                g.tensor_tensor(y[:, i, :], gam[:, q, :], vec[:, row + 1, :], ALU.add).then_inc(sm[pre + "y"], 1)

            wait(pool, "vec_in", 16)
            for i in range(NT + 1):
                if i < NC:
                    stage_scale(i)
                if i:
                    ln_rstd("s_", i - 1, (i - 1) % 2)
                    ln_affine("s_", i - 1, (i - 1) % 2, 0)
                if i < NC:
                    stage_lo(i)

            def q_stage(t, q):
                if isinstance(t, int) and t < 2:
                    pass
                else:
                    pool.wait_ge(sm["c_qtr"], t - 1)
                g.tensor_copy(qst[:, q, :], y[:, t, :]).then_inc(sm["c_qst"], 1)

            wait(pool, "s_y", NT)
            q_stage(0, 0)
            q_stage(1, 1)
            with pool.Fori(0, NT - 3, 2) as i:
                for q in range(2):
                    q_stage(i + q + 2, q)
                    ln_rstd("c_", i + q, q)
                    ln_affine("c_", i + q, q, 2)
            for i in (NT - 2, NT - 1):
                ln_rstd("c_", i, i % 2)
                ln_affine("c_", i, i % 2, 2)
            wait(pool, "c_y", NT)

            def y_stage(j):
                g.tensor_copy(yst[:], y[:, bass.ds(j * TB, TB), :]).then_inc(sm["f_yst"], 1)

            y_stage(0)

            def tail(j, m):
                i, q = j * TB + m, m % 2
                bridge_pool()
                g.tensor_tensor(y[:, i, :], y[:, i, :], vec[:, 6, :], ALU.add).then_inc(sm["n_yb"], 1)
                ln_rstd("n_", i, q)
                pool.wait_ge(sm["n_nrm"], i + 1)
                g.tensor_tensor(gam[:, q, :], nrm[:, q, :], vec[:, 4, :], ALU.mult).then_inc(sm["n_gam"], 1)
                pool.wait_ge(sm["n_gam"], i + 1)
                g.tensor_tensor(gam[:, q, :], gam[:, q, :], vec[:, 5, :], ALU.add).then_inc(sm["n_y3"], 1)
                pool.wait_ge(sm["n_y3"], i + 1)
                pool.wait_ge(sm["x2_in" + str(q)], 8 * (i - q) + 16)
                bridge_pool()
                g.tensor_tensor(y[:, i, :], gam[:, q, :], xin[:, q, :], ALU.add).then_inc(sm["x1_done"], 1)
                pool.wait_ge(sm["m_var"], i + 1)
                g.tensor_tensor(rstd[:, q, :], veps[:, q, :], expo[:], ALU.pow).then_inc(sm["m_rstd"], 1)

            with pool.Fori(0, NB - 1) as j:
                pool.wait_ge(sm["f_ytr"], j + 1)
                y_stage(j + 1)
                for m in range(TB):
                    tail(j, m)
            for m in range(TB):
                tail(NB - 1, m)

            for e in range(NE):
                wait(pool, "e_in", 16 * (e + 1))
                g.tensor_scalar(stage[:], stage[:], WS, None, ALU.mult).then_inc(sm["e_scaled"], 1)
                wait(pool, "e_hi", e + 1)
                g.tensor_tensor(ew[:, e % 2, 1, :], stage[:], ew[:, e % 2, 0, :], ALU.subtract).then_inc(sm["e_lo"], 1)

        @block.scalar
        def _(act_):
            a = nc.scalar

            def copy(o, i):
                return a.activation(o, i, ACT.Copy)

            with act_.Fori(0, NT - 1, 2) as i:
                for q in range(2):
                    t = i + q
                    act_.wait_ge(sm["l0_nrm"], t + 1)
                    copy(yv[:, 0, t, :], nrm[:, q, :]).then_inc(sm["l0_vhi"], 1)
                    act_.wait_ge(sm["l0_tr"], t + 1)
                    copy(yT[:, 0, :, t, :], psT[q][:, :D].rearrange("p (k t) -> p k t", k=KD)).then_inc(sm["l0_hi"], 1)

            def stage_hi(n):
                _, src, dst, _, _ = chunks[n]
                wait(act_, "stage_scaled", n + 1)
                copy(dst[:, 0], src).then_inc(sm["stage_hi"], 1)

            def exps(pre, q, count, c, w, n):
                act_.wait_ge(sm[pre + "bias"], count)
                a.activation(prob[:, q, c * CH:c * CH + w], ps[c][:, :w], ACT.Exp, bias=nbias[:, q, :], scale=SM,
                             accum_out=esum[:, q, c:c + 1]).then_inc(sm[pre + "exp"], 1)

            grp = [0]

            def s_his(i, g):
                n = min(4, i + 1 - 4 * g)
                grp[0] += 1
                wait(act_, "s_tr", grp[0])
                copy(probT[:, i % 2, 0, 4 * g:4 * g + n, :],
                     psT[(grp[0] - 1) % 2][:, :n * P].rearrange("p (k t) -> p k t", k=n)).then_inc(sm["s_hi"], 1)

            def s_exps(i, c):
                exps("s_", i % 2, i + 1, c, min(CH, (i + 1) * P - c * CH), 0)

            s_exps(0, 0)
            nst = 0
            for i in range(NT):
                ng = chunk_of(i)
                nch = chunk_of(i + 1) if i + 1 < NT else 0
                for g in range(min(2, ng)):
                    s_his(i, g)
                for c in range(min(2, nch)):
                    s_exps(i + 1, c)
                if ng > 2:
                    s_his(i, 2)
                for c in range(2, nch):
                    s_exps(i + 1, c)
                if ng > 3:
                    s_his(i, 3)
                if nst < NC:
                    stage_hi(nst)
                    nst += 1
            assert nst == NC

            def q_hi(t, q, k):
                act_.wait_ge(sm["c_qtr"], t + 1)
                copy(qT[:, q, 0, :, :], psT[k][:, P:P + D].rearrange("p (k t) -> p k t", k=KD)).then_inc(sm["c_qhi"], 1)

            def c_his(i, q, g, nxt2=False):
                act_.wait_ge(sm["c_tr"], 4 * i + g + 1)
                if nxt2:
                    act_.wait_ge(sm["c_qtr"], i + 3)
                n = 4 if g < 3 else 1
                r = P if g < 3 else ZR
                copy(probT[:r, q, 0, 4 * g:4 * g + n, :],
                     psT[g % 2][:r, :n * P].rearrange("p (k t) -> p k t", k=n)).then_inc(sm["c_hi"], 1)

            def c_exps(t, q, c):
                exps("c_", q, t + 1, c, CW[c], 0)

            q_hi(0, 0, 0)
            q_hi(1, 1, 1)
            for c in range(C_CH):
                c_exps(0, 0, c)

            def c_step(i, q, nxt, nxt2):
                c_his(i, q, 0)
                c_his(i, q, 1)
                if nxt:
                    c_exps(i + 1, 1 - q, 0)
                    c_exps(i + 1, 1 - q, 1)
                c_his(i, q, 2)
                if nxt:
                    c_exps(i + 1, 1 - q, 2)
                    c_exps(i + 1, 1 - q, 3)
                c_his(i, q, 3, nxt2)
                if nxt2:
                    q_hi(i + 2, q, 1)

            with act_.Fori(0, NT - 3, 2) as i:
                c_step(i, 0, True, True)
                c_step(i + 1, 1, True, True)
            c_step(NT - 2, 0, True, False)
            c_step(NT - 1, 1, False, False)

            def y_hi(j):
                for k in range(KD):
                    act_.wait_ge(sm["f_ytr"], j + 1)
                    copy(ybT[:, 0, k, :], psT[k][:]).then_inc(sm["f_yhi"], 1)

            def relus(j):
                for f in range(KF):
                    act_.wait_ge(sm["f_up"], j * KF + f + 1)
                    if f >= 2:
                        act_.wait_ge(sm["f_lo"], j * KF + f - 1)
                    a.activation(hid[:, f % 2, :], ps[f % 2][:], ACT.Relu, bias=b1c[:, f:f + 1],
                                 scale=1.0 / WS).then_inc(sm["f_relu"], 1)

            def h_parts(i, q):
                act_.wait_ge(sm["h_tr"], i + 1)
                copy(yT[:, 0, :, i, :], ps[2 + q][:, :D].rearrange("p (k t) -> p k t", k=KD)).then_inc(sm["h_hi"], 1)

            def gates(i, q):
                act_.wait_ge(sm["r_dl"], i + 1)
                a.activation(gt[:, q, 0:1], dl[:, q, :], ACT.Exp).then_inc(sm["r_exp"], 1)

            wait(act_, "b1_in", 16)
            y_hi(0)
            relus(0)
            with act_.Fori(0, NB - 1) as j:
                y_hi(j + 1)
                for m in range(TB):
                    h_parts(j * TB + m, m % 2)
                    gates(j * TB + m, m % 2)
                relus(j + 1)
            for m in range(TB):
                h_parts((NB - 1) * TB + m, m % 2)
                gates((NB - 1) * TB + m, m % 2)

            def e_his(e):
                wait(act_, "e_scaled", e + 1)
                if e >= 2:
                    wait(act_, "e_down", NT * (e - 1))
                copy(ew[:, e % 2, 0, :], stage[:]).then_inc(sm["e_hi"], 1)

            e_his(0)

            def silus(n, q):
                act_.wait_ge(sm["e_up"], n + 1)
                a.activation(sil[:, q, :], ps[2 * q][:], ACT.Silu, scale=1.0 / WS).then_inc(sm["e_sil"], 1)

            def act_hi(n, q):
                act_.wait_ge(sm["e_tr"], n + 1)
                copy(actT[:, q, 0, :, :].rearrange("p k t -> p (k t)"), psT[q][:]).then_inc(sm["e_ahi"], 1)

            for e in range(NE):
                silus(e * NT, 0)
                if e + 1 < NE:
                    e_his(e + 1)
                with act_.Fori(0, NT - 3, 2) as i:
                    silus(i + (e * NT + 1), 1)
                    act_hi(i + e * NT, 0)
                    silus(i + (e * NT + 2), 0)
                    act_hi(i + (e * NT + 1), 1)
                silus(e * NT + NT - 1, 1)
                act_hi(e * NT + NT - 2, 0)
                act_hi(e * NT + NT - 1, 1)

        @block.tensor
        def _(pe):
            t = nc.tensor

            def mm3(o, lhs, rhs, first, last):
                for n, (a, b) in enumerate(PARTS):
                    r = t.matmul(o, lhs(a), rhs(b), start=first and n == 0, stop=last and n == 2)
                return r

            wait(pe, "consts", 8)
            with pe.Fori(0, NT - 1, 2) as i:
                for q in range(2):
                    pe.wait_ge(sm["l0_nrm"], i + q + 1)
                    pe.wait_ge(sm["l0_lo"], i + q + 1)
                    for k in range(KD):
                        r = t.transpose(psT[q][:, k * P:(k + 1) * P], nrm[:, q, k * P:(k + 1) * P], ident[:])
                    r.then_inc(sm["l0_tr"], 1)
            wait(pe, "l0_lo", NT + 2)
            wait(pe, "l0_vlo", NT)

            grp = [0]

            def s_scores(i):
                n = chunk_of(i)
                for c in range(n):
                    w = min(CH, (i + 1) * P - c * CH)
                    prev = [j for j in range(i) if chunk_of(j) > c]
                    if prev:
                        wait(pe, "s_exp", S_CH[prev[-1]] + c + 1)
                    o = ps[c][:, :w]
                    diag = c == n - 1
                    for k in range(KD):
                        r = mm3(o, lambda a: yT[:, a, k, i, :],
                                lambda b: yT[:, b, k, 4 * c:4 * c + w // P, :],
                                k == 0, k == KD - 1 and not diag)
                    if diag:
                        r = t.matmul(ps[c][:, w - P:w], ident16[:], mask[:], start=False, stop=True)
                    r.then_inc(sm["s_scores"], 1)

            def s_trans(i, g):
                grp[0] += 1
                k = grp[0] - 1
                if k >= 2:
                    wait(pe, "s_lo", k - 1)
                if g == 0:
                    wait(pe, "s_exp", S_CH[i + 1])
                n = min(4, i + 1 - 4 * g)
                for m in range(n):
                    r = t.transpose(psT[k % 2][:, m * P:(m + 1) * P],
                                    prob[:, i % 2, (4 * g + m) * P:(4 * g + m + 1) * P], ident[:])
                r.then_inc(sm["s_tr"], 1)

            def s_pv(i, g):
                wait(pe, "s_lo", S_CH[i] + g + 1)
                if g == 0 and i >= 2:
                    wait(pe, "s_u", i - 1)
                for m in range(4 * g, min(4 * g + 4, i + 1)):
                    r = mm3(psO[i % 2][:, :D], lambda a: probT[:, i % 2, a, m, :], lambda b: yv[:, b, m, :],
                            m == 0, m == i)
                if 4 * g + 4 >= i + 1:
                    r.then_inc(sm["s_pv"], 1)

            s_scores(0)
            for i in range(NT):
                ng = chunk_of(i)
                for g in range(min(2, ng)):
                    s_trans(i, g)
                if i + 1 < NT:
                    s_scores(i + 1)
                for g in range(ng):
                    s_pv(i, g)
                    if g + 2 < ng:
                        s_trans(i, g + 2)

            def q_trans(i, q, k):
                pe.wait_ge(sm["c_qst"], i + 1)
                for m in range(KD):
                    r = t.transpose(psT[k][:, (m + 1) * P:(m + 2) * P], qst[:, q, m * P:(m + 1) * P], ident[:])
                r.then_inc(sm["c_qtr"], 1)

            def c_scores(i, q, first):
                pe.wait_ge(sm["c_qlo"], i + 1)
                for c in range(C_CH):
                    if not first:
                        pe.wait_ge(sm["c_exp"], 4 * i + (c - 3))
                    w = CW[c]
                    for k in range(KD):
                        r = mm3(ps[c][:, :w], lambda a: qT[:, q, a, k, :],
                                lambda b: zTs[:, b, k, c * CH:c * CH + w], k == 0, k == KD - 1)
                    r.then_inc(sm["c_scores"], 1)

            def c_trans(i, q, g, first=False):
                if g < 2:
                    if not first:
                        pe.wait_ge(sm["c_lo"], 4 * i + g - 1)
                        if g == 1:
                            pe.wait_ge(sm["c_qlo"], min(i + 2, NT) if isinstance(i, int) else i + 2)
                else:
                    pe.wait_ge(sm["c_lo"], 4 * i + g - 1)
                if g == 0:
                    pe.wait_ge(sm["c_exp"], 4 * i + 4)
                for m in range(4 * g, min(4 * g + 4, NZ)):
                    r_ = P if m < NZ - 1 else ZR
                    r = t.transpose(psT[g % 2][:r_, (m % 4) * P:(m % 4 + 1) * P],
                                    prob[:, q, m * P:m * P + r_], ident[:])
                r.then_inc(sm["c_tr"], 1)

            def c_pv(i, q, g, first=False):
                pe.wait_ge(sm["c_lo"], 4 * i + g + 1)
                if g == 0 and not first:
                    pe.wait_ge(sm["c_u"], i - 1)
                for m in range(4 * g, min(4 * g + 4, NZ)):
                    r_ = P if m < NZ - 1 else ZR
                    r = mm3(psO[q][:, :D], lambda a: probT[:r_, q, a, m, :], lambda b: zs[:r_, b, m, :],
                            m == 0, m == NZ - 1)
                if g == 3:
                    r.then_inc(sm["c_pv"], 1)

            wait(pe, "stage_lo", NC)
            wait(pe, "s_lo", grp[0])
            wait(pe, "s_exp", S_CH[NT])
            wait(pe, "s_u", NT)
            q_trans(0, 0, 0)
            q_trans(1, 1, 1)
            c_scores(0, 0, True)

            def c_step(i, q, nxt, nxt2, first=False):
                c_trans(i, q, 0, first)
                c_trans(i, q, 1, first)
                if nxt:
                    c_scores(i + 1, 1 - q, False)
                c_pv(i, q, 0, first)
                c_trans(i, q, 2)
                c_pv(i, q, 1, first)
                c_trans(i, q, 3)
                if nxt2:
                    q_trans(i + 2, q, 1)
                c_pv(i, q, 2)
                c_pv(i, q, 3)

            c_step(0, 0, True, True, True)
            c_step(1, 1, True, True, True) if False else None
            wait(pe, "c_lo", 3)
            c_trans(1, 1, 0)
            c_trans(1, 1, 1)
            c_scores(2, 0, False)
            c_pv(1, 1, 0, True)
            c_trans(1, 1, 2)
            c_pv(1, 1, 1)
            c_trans(1, 1, 3)
            q_trans(3, 1, 1)
            c_pv(1, 1, 2)
            c_pv(1, 1, 3)
            with pe.Fori(2, NT - 3, 2) as i:
                c_step(i, 0, True, True)
                c_step(i + 1, 1, True, True)
            c_step(NT - 2, 0, True, False)
            c_step(NT - 1, 1, False, False)

            wait(pe, "c_lo", 4 * NT)
            wait(pe, "c_exp", 4 * NT)
            wait(pe, "c_u", NT)

            def y_trans(j):
                pe.wait_ge(sm["f_yst"], j + 1)
                for k in range(KD):
                    for m in range(TB):
                        r = t.transpose(psT[k][:, m * P:(m + 1) * P], yst[:, m, k * P:(k + 1) * P], ident[:])
                r.then_inc(sm["f_ytr"], 1)

            def ups(j, first):
                pe.wait_ge(sm["f_ylo"], KD * j + KD)
                for f in range(KF):
                    if f >= 2 or not first:
                        pe.wait_ge(sm["f_relu"], KF * j + f - 1)
                    for k in range(KD):
                        r = mm3(ps[f % 2][:], lambda a: w1s[:, a, k, f * P:(f + 1) * P], lambda b: ybT[:, b, k, :],
                                k == 0, k == KD - 1)
                    r.then_inc(sm["f_up"], 1)

            def down(j, m, first):
                if m == 0:
                    pe.wait_ge(sm["f_lo"], KF * j + KF)
                i = j * TB + m
                if m >= 2 or not first:
                    pe.wait_ge(sm["n_u"], i - 1)
                for f in range(KF):
                    r = mm3(psO[m % 2][:, :D], lambda a: hidT[:, a, f, m * P:(m + 1) * P], lambda b: w2s[:, b, f, :],
                            f == 0, f == KF - 1)
                r.then_inc(sm["f_down"], 1)

            def h_and_logits(j, m):
                i, q = j * TB + m, m % 2
                pe.wait_ge(sm["m_nrm"], i + 1)
                for k in range(KD):
                    r = t.transpose(ps[2 + q][:, k * P:(k + 1) * P], nrm[:, q, k * P:(k + 1) * P], ident[:])
                r.then_inc(sm["h_tr"], 1)
                pe.wait_ge(sm["h_lo"], i + 1)
                for k in range(KD):
                    r = mm3(ps[2 + q][:, D:D + NE], lambda a: yT[:, a, k, i, :], lambda b: wgs[:, b, k, :],
                            k == 0, k == KD - 1)
                r.then_inc(sm["r_logit"], 1)

            y_trans(0)
            ups(0, True)
            y_trans(1)
            down(0, 0, True)
            down(0, 1, True)
            h_and_logits(0, 0)
            down(0, 2, True)
            h_and_logits(0, 1)
            down(0, 3, True)
            h_and_logits(0, 2)
            h_and_logits(0, 3)
            with pe.Fori(1, NB - 1) as j:
                ups(j, False)
                y_trans(j + 1)
                down(j, 0, False)
                for m in range(1, TB):
                    down(j, m, False)
                    h_and_logits(j, m - 1)
                h_and_logits(j, TB - 1)
            ups(NB - 1, False)
            for m in range(TB):
                down(NB - 1, m, False)
                if m:
                    h_and_logits(NB - 1, m - 1)
            h_and_logits(NB - 1, TB - 1)

            wait(pe, "r_lg", NT)
            wait(pe, "n_u", NT)

            def e_ups(e, i, q, n, first=False):
                if not first:
                    pe.wait_ge(sm["e_act"], n - 1)
                for h in range(2):
                    for k in range(KD):
                        r = mm3(ps[2 * q + h][:], lambda a: yT[:, a, k, i, :],
                                lambda b: ew[:, e % 2, b, k * 2 * NI + h * NI:k * 2 * NI + (h + 1) * NI],
                                k == 0, k == KD - 1)
                r.then_inc(sm["e_up"], 1)

            def e_trans(n, q, first=False):
                pe.wait_ge(sm["e_act"], n + 1)
                if not first:
                    pe.wait_ge(sm["e_alo"], n - 1)
                for k in range(KI):
                    r = t.transpose(psT[q][:, k * P:(k + 1) * P], act[:, q, k * P:(k + 1) * P], ident[:])
                r.then_inc(sm["e_tr"], 1)

            def e_downs(e, n, q, first=False):
                pe.wait_ge(sm["e_alo"], n + 1)
                if not first:
                    pe.wait_ge(sm["e_acc"], n - 1)
                for k in range(KI):
                    r = mm3(psO[q][:, :D], lambda a: actT[:, q, a, k, :],
                            lambda b: ew[:, e % 2, b, 2 * KD * NI + k * D:2 * KD * NI + (k + 1) * D],
                            k == 0, k == KI - 1)
                r.then_inc(sm["e_down"], 1)

            for e in range(NE):
                n0 = e * NT
                wait(pe, "e_lo", e + 1)
                f = e == 0
                e_ups(e, 0, 0, n0, f)
                e_ups(e, 1, 1, n0 + 1, f)
                e_trans(n0, 0, f)
                e_ups(e, 2, 0, n0 + 2)
                e_trans(n0 + 1, 1, f)
                e_downs(e, n0, 0, f)
                e_ups(e, 3, 1, n0 + 3)
                e_trans(n0 + 2, 0)
                e_downs(e, n0 + 1, 1, f)
                with pe.Fori(4, NT - 1, 2) as i:
                    e_ups(e, i, 0, i + n0)
                    e_trans(i + (n0 - 1), 1)
                    e_downs(e, i + (n0 - 2), 0)
                    e_ups(e, i + 1, 1, i + (n0 + 1))
                    e_trans(i + n0, 0)
                    e_downs(e, i + (n0 - 1), 1)
                e_trans(n0 + NT - 1, 1)
                e_downs(e, n0 + NT - 2, 0)
                e_downs(e, n0 + NT - 1, 1)

        @block.vector
        def _(dve):
            v = nc.vector

            def step(name):
                return lambda ins, count: (ins.then_inc(sm[name], 1), dve.wait_ge(sm[name], count))

            def moments(pre, src, q, i):
                v.bn_stats(stat[:, q, :], src).then_inc(sm[pre + "stat"], 1)
                dve.wait_ge(sm[pre + "stat"], i + 1)
                bridge_dve()
                v.bn_aggr(mv[:, q, :], stat[:, q, :]).then_inc(sm[pre + "agg"], 1)
                dve.wait_ge(sm[pre + "agg"], i + 1)
                v.tensor_scalar(veps[:, q, :], mv[:, q, 1:2], EPS, None, ALU.add).then_inc(sm[pre + "var"], 1)

            def normalise(pre, src, q, i):
                dve.wait_ge(sm[pre + "rstd"], i + 1)
                v.tensor_scalar(nrm[:, q, :], src, mv[:, q, 0:1], rstd[:, q, :], ALU.subtract,
                                ALU.mult).then_inc(sm[pre + "nrm"], 1)

            v.memset(topf[:, 0, 0:1], 0.0).then_inc(sm["l0_lo"], 2)
            with dve.Fori(0, NT - 1, 2) as i:
                for q in range(2):
                    t = i + q
                    dve.wait_ge(sm["x_in" + str(q)], 8 * i + 16)
                    moments("l0_", xin[:, q, :], q, t)
                    dve.wait_ge(sm["l0_lo"], t + 1)
                    normalise("l0_", xin[:, q, :], q, t)
                    dve.wait_ge(sm["l0_hi"], t + 1)
                    v.tensor_tensor(yT[:, 1, :, t, :], psT[q][:, :D].rearrange("p (k t) -> p k t", k=KD),
                                    yT[:, 0, :, t, :], ALU.subtract).then_inc(sm["l0_lo"], 1)
                    dve.wait_ge(sm["l0_vlo"], t + 1)
                    dve.wait_ge(sm["l0_copy"], t + 1)

            def maxes(pre, q, c, w, count, scores):
                dve.wait_ge(sm[pre + "scores"], scores)
                v.tensor_reduce(cmax[:, q, c:c + 1], ps[c][:, :w], X, ALU.max).then_inc(sm[pre + "cmax"], 1)

            def bias(pre, q, n, i, count):
                dve.wait_ge(sm[pre + "cmax"], count)
                v.tensor_reduce(nmax[:, q, :], cmax[:, q, :n], X, ALU.max, negate=True).then_inc(sm[pre + "nmax"], 1)
                dve.wait_ge(sm[pre + "nmax"], i + 1)
                v.tensor_scalar(nbias[:, q, :], nmax[:, q, :], SM, None, ALU.mult).then_inc(sm[pre + "bias"], 1)

            def sums(pre, q, n, i, count):
                dve.wait_ge(sm[pre + "exp"], count)
                v.tensor_reduce(rsum[:, q, :], esum[:, q, :n], X, ALU.add).then_inc(sm[pre + "rsum"], 1)
                dve.wait_ge(sm[pre + "rsum"], i + 1)
                v.reciprocal(rinv[:, q, :], rsum[:, q, :]).then_inc(sm[pre + "rinv"], 1)

            def residual(pre, i, q):
                dve.wait_ge(sm[pre + "rinv"], i + 1)
                dve.wait_ge(sm[pre + "pv"], i + 1)
                v.scalar_tensor_tensor(u[:, q, :], psO[q][:, :D], rinv[:, q, :], y[:, i, :], ALU.mult,
                                       ALU.add).then_inc(sm[pre + "u"], 1)
                dve.wait_ge(sm[pre + "u"], i + 1)
                moments(pre, u[:, q, :], q, i)

            grp = [0]

            def s_los(i, g):
                n = min(4, i + 1 - 4 * g)
                grp[0] += 1
                wait(dve, "s_hi", grp[0])
                k = (grp[0] - 1) % 2
                v.tensor_tensor(probT[:, i % 2, 1, 4 * g:4 * g + n, :],
                                psT[k][:, :n * P].rearrange("p (k t) -> p k t", k=n),
                                probT[:, i % 2, 0, 4 * g:4 * g + n, :], ALU.subtract).then_inc(sm["s_lo"], 1)

            def s_max(i):
                for c in range(chunk_of(i)):
                    maxes("s_", i % 2, c, min(CH, (i + 1) * P - c * CH), 0, S_CH[i] + c + 1)
                bias("s_", i % 2, chunk_of(i), i, S_CH[i + 1])

            def s_norm(i):
                if i >= 2:
                    wait(dve, "s_gam", i - 1)
                normalise("s_", u[:, i % 2, :], i % 2, i)

            s_max(0)
            for i in range(NT):
                ng = chunk_of(i)
                for g in range(min(2, ng)):
                    s_los(i, g)
                if i:
                    residual("s_", i - 1, (i - 1) % 2)
                if i + 1 < NT:
                    s_max(i + 1)
                if i:
                    s_norm(i - 1)
                sums("s_", i % 2, ng, i, S_CH[i + 1])
                for g in range(2, ng):
                    s_los(i, g)
            residual("s_", NT - 1, (NT - 1) % 2)
            s_norm(NT - 1)

            def q_lo(t, q, k):
                dve.wait_ge(sm["c_qhi"], t + 1)
                v.tensor_tensor(qT[:, q, 1, :, :], psT[k][:, P:P + D].rearrange("p (k t) -> p k t", k=KD),
                                qT[:, q, 0, :, :], ALU.subtract).then_inc(sm["c_qlo"], 1)

            def c_los(i, q, g, nxt2=False):
                n = 4 if g < 3 else 1
                r = P if g < 3 else ZR
                dve.wait_ge(sm["c_hi"], 4 * i + g + 1)
                if nxt2:
                    dve.wait_ge(sm["c_qhi"], i + 3)
                v.tensor_tensor(probT[:r, q, 1, 4 * g:4 * g + n, :],
                                psT[g % 2][:r, :n * P].rearrange("p (k t) -> p k t", k=n),
                                probT[:r, q, 0, 4 * g:4 * g + n, :], ALU.subtract).then_inc(sm["c_lo"], 1)

            def c_max(i, q):
                for c in range(C_CH):
                    maxes("c_", q, c, CW[c], 0, 4 * i + c + 1)
                bias("c_", q, C_CH, i, 4 * i + 4)

            def c_norm(i, q, first=False):
                if not first:
                    dve.wait_ge(sm["c_gam"], i - 1)
                normalise("c_", u[:, q, :], q, i)

            def c_step(i, q, nxt, nxt2, prev=2):
                c_los(i, q, 0)
                c_los(i, q, 1)
                if prev:
                    residual("c_", i - 1, 1 - q)
                if nxt:
                    c_max(i + 1, 1 - q)
                if prev:
                    c_norm(i - 1, 1 - q, prev == 1)
                sums("c_", q, C_CH, i, 4 * i + 4)
                c_los(i, q, 2)
                c_los(i, q, 3, nxt2)
                if nxt2:
                    q_lo(i + 2, q, 1)

            wait(dve, "s_gam", NT)
            q_lo(0, 0, 0)
            q_lo(1, 1, 1)
            c_max(0, 0)
            c_step(0, 0, True, True, 0)
            c_step(1, 1, True, True, 1)
            c_step(2, 0, True, True, 1)
            c_step(3, 1, True, True)
            with dve.Fori(4, NT - 3, 2) as i:
                c_step(i, 0, True, True)
                c_step(i + 1, 1, True, True)
            c_step(NT - 2, 0, True, False)
            c_step(NT - 1, 1, False, False)
            residual("c_", NT - 1, 1)
            c_norm(NT - 1, 1)
            wait(dve, "c_gam", NT)

            def y_lo(j):
                for k in range(KD):
                    dve.wait_ge(sm["f_yhi"], KD * j + k + 1)
                    v.tensor_tensor(ybT[:, 1, k, :], psT[k][:], ybT[:, 0, k, :], ALU.subtract).then_inc(sm["f_ylo"], 1)

            def hid_parts(j):
                for f in range(KF):
                    dve.wait_ge(sm["f_relu"], KF * j + f + 1)
                    v.tensor_copy(hidT[:, 0, f, :], hid[:, f % 2, :]).then_inc(sm["f_hi"], 1)
                    dve.wait_ge(sm["f_hi"], KF * j + f + 1)
                    v.tensor_tensor(hidT[:, 1, f, :], hid[:, f % 2, :], hidT[:, 0, f, :],
                                    ALU.subtract).then_inc(sm["f_lo"], 1)

            def tail(j, m):
                i, q = j * TB + m, m % 2
                dve.wait_ge(sm["f_down"], i + 1)
                dve.wait_ge(sm["n_yb"], i + 1)
                v.scalar_tensor_tensor(u[:, q, :], psO[q][:, :D], 1.0 / WS, y[:, i, :], ALU.mult,
                                       ALU.add).then_inc(sm["n_u"], 1)
                dve.wait_ge(sm["n_u"], i + 1)
                moments("n_", u[:, q, :], q, i)
                normalise("n_", u[:, q, :], q, i)
                dve.wait_ge(sm["x1_done"], i + 2)
                bridge_dve()
                v.bn_stats(stat[:, q, :], y[:, i, :]).then_inc(sm["m_stat"], 1)
                dve.wait_ge(sm["m_stat"], i + 1)
                bridge_dve()
                v.bn_aggr(mv[:, q, :], stat[:, q, :]).then_inc(sm["m_agg"], 1)
                dve.wait_ge(sm["m_agg"], i + 1)
                v.tensor_scalar(veps[:, q, :], mv[:, q, 1:2], EPS, None, ALU.add).then_inc(sm["m_var"], 1)
                normalise("m_", y[:, i, :], q, i)

            def route(j, m):
                i, q = j * TB + m, m % 2
                n = i + 1
                dve.wait_ge(sm["h_hi"], n)
                v.tensor_tensor(yT[:, 1, :, i, :], ps[2 + q][:, :D].rearrange("p (k t) -> p k t", k=KD),
                                yT[:, 0, :, i, :], ALU.subtract).then_inc(sm["h_lo"], 1)
                dve.wait_ge(sm["r_logit"], n)
                step("r_lg")(v.tensor_scalar(lg[:, q, :], ps[2 + q][:, D:D + NE], 1.0 / WS, None, ALU.mult), n)
                bridge_dve()
                step("r_top")(v.max(top[:, q, :], lg[:, q, :]), n)
                bridge_dve()
                v.max_index(topi[:, q, :], top[:, q, :], lg[:, q, :]).then_inc(sm["r_topi"], 1)
                v.tensor_tensor(dl[:, q, :], top[:, q, 1:2], top[:, q, 0:1], ALU.subtract).then_inc(sm["r_dl"], 1)
                dve.wait_ge(sm["r_topi"], n)
                step("r_topf")(v.tensor_copy(topf[:, q, :], topi[:, q, 0:2]), n)
                for c in range(2):
                    v.tensor_scalar(oh[:, q, c, :], iota8[:], topf[:, q, c:c + 1], None,
                                    ALU.is_equal).then_inc(sm["r_oh"], 1)
                dve.wait_ge(sm["r_exp"], n)
                step("r_den")(v.tensor_scalar(gt[:, q, 1:2], gt[:, q, 0:1], 1.0, None, ALU.add), n)
                step("r_w1")(v.reciprocal(gt[:, q, 2:3], gt[:, q, 1:2]), n)
                step("r_w2")(v.tensor_tensor(gt[:, q, 3:4], gt[:, q, 0:1], gt[:, q, 2:3], ALU.mult), n)
                dve.wait_ge(sm["r_oh"], 2 * n)
                step("r_g1")(v.tensor_scalar(oh[:, q, 0, :], oh[:, q, 0, :], gt[:, q, 2:3], None, ALU.mult), n)
                v.scalar_tensor_tensor(gate[:, i, :], oh[:, q, 1, :], gt[:, q, 3:4], oh[:, q, 0, :], ALU.mult,
                                       ALU.add).then_inc(sm["r_gate"], 1)

            def tails(j):
                tail(j, 0)
                for m in range(1, TB):
                    tail(j, m)
                    route(j, m - 1)
                route(j, TB - 1)

            y_lo(0)
            hid_parts(0)
            with dve.Fori(0, NB - 1) as j:
                y_lo(j + 1)
                tails(j)
                hid_parts(j + 1)
            tails(NB - 1)
            wait(dve, "r_gate", NT)

            def gated(n, q, first=False):
                dve.wait_ge(sm["e_sil"], n + 1)
                v.scalar_tensor_tensor(act[:, q, :], ps[2 * q + 1][:], 1.0 / WS, sil[:, q, :], ALU.mult,
                                       ALU.mult).then_inc(sm["e_act"], 1)

            def act_lo(n, q):
                dve.wait_ge(sm["e_ahi"], n + 1)
                v.tensor_tensor(actT[:, q, 1, :, :].rearrange("p k t -> p (k t)"), psT[q][:],
                                actT[:, q, 0, :, :].rearrange("p k t -> p (k t)"), ALU.subtract).then_inc(sm["e_alo"], 1)

            def add_up(e, i, n, q):
                dve.wait_ge(sm["e_down"], n + 1)
                v.scalar_tensor_tensor(y[:, i, :], psO[q][:, :D], gate[:, i, e:e + 1], y[:, i, :], ALU.mult,
                                       ALU.add).then_inc(sm["e_acc"], 1)

            v.tensor_scalar(gate[:], gate[:], 1.0 / WS, None, ALU.mult).then_inc(sm["r_gate"], 1)
            wait(dve, "r_gate", NT + 1)
            for e in range(NE):
                n0 = e * NT
                gated(n0, 0)
                gated(n0 + 1, 1)
                act_lo(n0, 0)
                with dve.Fori(2, NT - 1, 2) as i:
                    gated(i + n0, 0)
                    act_lo(i + (n0 - 1), 1)
                    add_up(e, i - 2, i + (n0 - 2), 0)
                    gated(i + (n0 + 1), 1)
                    act_lo(i + n0, 0)
                    add_up(e, i - 1, i + (n0 - 1), 1)
                act_lo(n0 + NT - 1, 1)
                add_up(e, NT - 2, n0 + NT - 2, 0)
                add_up(e, NT - 1, n0 + NT - 1, 1)


def kernel(**inputs):
    import concourse.bacc as bacc
    from concourse.bass_utils import run_bass_kernel_spmd

    a = {k: np.asarray(v) for k, v in inputs.items()}
    f = "L0_xattn_"
    ctx_ = a["ctx_1024"][0]
    w13 = np.concatenate([a["L0_ffn_w1"].transpose(0, 2, 1), a["L0_ffn_w3"].transpose(0, 2, 1)], axis=2)
    w13 = w13.reshape(NE, KD, P, 2 * NI).transpose(0, 2, 1, 3).reshape(NE, P, KD * 2 * NI)
    w2t = a["L0_ffn_w2"].transpose(0, 2, 1).reshape(NE, KI, P, D).transpose(0, 2, 1, 3).reshape(NE, P, KI * D)
    arrays = {
        "x_in": a["x"][0],
        "z_in": ctx_,
        "zT_in": ctx_.T,
        "w1_in": a[f + "w1"],
        "w2_in": a[f + "w2"],
        "wgT_in": a["L0_ffn_wg"].T,
        "we_in": np.concatenate([w13, w2t], axis=2),
        "b1_in": a[f + "b1"].reshape(KF, P).T,
        "rows_in": np.concatenate([a[f + n] for n in ("g1", "beta1", "g2", "beta2", "g3", "beta3", "b2")]),
    }
    arrays = {k: np.ascontiguousarray(v) for k, v in arrays.items()}
    nc = bacc.Bacc("TRN2", target_bir_lowering=False, num_devices=1)
    args = [nc.dram_tensor(k, v.shape, mybir.dt.from_np(v.dtype), kind="ExternalInput").ap()
            for k, v in arrays.items()]
    out = nc.dram_tensor("out", (S, D), F32, kind="ExternalOutput").ap()
    xattn_ffn_moe(nc, *args, out)
    r = run_bass_kernel_spmd(nc, [arrays], core_ids=[0])
    return r.results[0]["out"].reshape(1, S, D)
```

```python
import numpy as np
import concourse.bass as bass
from concourse import mybir
from contextlib import ExitStack

F32, F16, U32, I32 = mybir.dt.float32, mybir.dt.float16, mybir.dt.uint32, mybir.dt.int32
ALU = mybir.AluOpType
ACT = mybir.ActivationFunctionType
X = mybir.AxisListType.X

P = 128
S, D = 2048, 256
L = 1601
DFF = 1024
NE, NI = 8, 512
TOP = 2
NT = S // P
KD = D // P
NZ = -(-L // P)
ZR = L - (NZ - 1) * P
KF = DFF // P
KI = NI // P
CH = 4 * P
TB = 4
NB = NT // TB
EPS = 1e-5
WS = 64.0
SM = float(D) ** -0.5
MASKED = -60000.0
NP = KD * 2 + KI * D // CH
NJ = TOP * NT + NE
BL = NT
LISTS = (NE - 1) * BL + NJ
PW = 832

PARTS = ((0, 0), (0, 1), (1, 0))


def xattn_ffn_moe(nc, x, z, zT, w1, w2, wgT, we, b1, rows, out):
    with ExitStack() as ctx:
        def sb(name, shape, dt=F32):
            return ctx.enter_context(nc.sbuf_tensor(name, shape, dt))

        def sem(name):
            return ctx.enter_context(nc.semaphore(name))

        hrow = nc.dram_tensor("hrow", (S + P, 2 * D), F16, kind="Internal").ap()
        lists = nc.dram_tensor("lists", (LISTS * P, 2), U32, kind="Internal").ap()

        ident = sb("ident", [P, P])
        ident16 = sb("ident16", [P, P], F16)
        mask = sb("mask", [P, P], F16)
        tri = sb("tri", [P, P], F16)
        ones = sb("ones", [P, P], F16)
        expo = sb("expo", [P, TB])
        bridge = sb("bridge", [P, 3])
        iota8 = sb("iota8", [P, NE])
        ebase = sb("ebase", [P, NE])
        cuts = sb("cuts", [P, NT])
        tri8 = sb("tri8", [P, NE, NE])
        jot = sb("jot", [P, NJ])
        vec = sb("vec", [P, 5, D])
        b1c = sb("b1c", [P, KF])
        w1m = sb("w1m", [P, KD * DFF])
        w2s = sb("w2s", [P, 2, KF, D], F16)
        wgs = sb("wgs", [P, 2, KD, NE], F16)
        w1s = w1m[:].bitcast(F16).rearrange("p (a k f) -> p a k f", a=2, k=KD)
        arena = sb("arena", [P, NE * NP * 2 * CH], F16)
        ew = arena[:].rearrange("p (n a c) -> p n a c", a=2, c=CH)
        NA = NE * NP * 2 * CH
        yv = arena[:, :2 * NT * D].rearrange("p (a t d) -> p a t d", a=2, t=NT)
        z0 = NA - 2 * NZ * D - 2 * KD * L
        zs = arena[:, z0:z0 + 2 * NZ * D].rearrange("p (a t d) -> p a t d", a=2, t=NZ)
        zTs = arena[:, z0 + 2 * NZ * D:].rearrange("p (a k l) -> p a k l", a=2, k=KD)
        FREE0 = -(-2 * NT * D // (2 * CH))
        FREE1 = z0 // (2 * CH)
        y = sb("y", [P, NT, D])
        xin = sb("xin", [P, 2, TB, D])
        tT = sb("tT", [P, 2 * KD * NT * P], F16)
        yT = tT[:].rearrange("p (a k t c) -> p a k t c", a=2, k=KD, t=NT)
        hidT = tT[:].rearrange("p (a f c) -> p a f c", a=2, f=KF)
        prob = sb("prob", [P, 2, NT * P])
        probT = sb("probT", [P, 2, 2, NT, P], F16)
        stage = sb("stage", [P, 2, PW])
        pf = prob[:].rearrange("p a b -> p (a b)")
        hid = pf[:, 0:2 * CH].rearrange("p (q c) -> p q c", q=2)
        u4 = pf[:, 1024:2048].rearrange("p (m d) -> p m d", m=TB)
        n4 = pf[:, 2048:3072].rearrange("p (m d) -> p m d", m=TB)
        h4 = pf[:, 3072:4096].rearrange("p (m d) -> p m d", m=TB)
        ph = probT[:].rearrange("p s a t c -> p (s a t c)")
        ybT = ph[:, 0:2048].rearrange("p (a k c) -> p a k c", a=2, k=KD)
        hs = ph[:, 2048:4096].rearrange("p (m a d) -> p m a d", m=TB, a=2)
        hT = ph[:, 4096:6144].rearrange("p (m a k c) -> p m a k c", m=TB, a=2, k=KD)
        actT = tT[:, 0:2048].rearrange("p (q a k c) -> p q a k c", q=2, a=2, k=KI)
        xg = tT[:, 2048:3072].rearrange("p (q c) -> p q c", q=2)
        xT = tT[:, 3072:4096].rearrange("p (q b c) -> p q b c", q=2, b=2 * KD)
        sil = w1m[:, 0:2 * NI].rearrange("p (q c) -> p q c", q=2)
        act = w1m[:, 2 * NI:4 * NI].rearrange("p (q c) -> p q c", q=2)
        ys = stage[:, :, :D]
        qst = sb("qst", [P, 2, D])
        qT = sb("qT", [P, 2, 2, KD, P], F16)
        zero = qT[:].rearrange("p q a k c -> p (q a k c)")[:, :2 * D]
        u = sb("u", [P, 2, D])
        nrm = sb("nrm", [P, 2, D])
        cmax = sb("cmax", [P, 2, 4])
        nmax = sb("nmax", [P, 2, 1])
        nbias = sb("nbias", [P, 2, 1])
        esum = sb("esum", [P, 2, 4])
        rsum = sb("rsum", [P, 2, 1])
        rinv = sb("rinv", [P, 2, 1])
        stat = sb("stat", [P, 2, 6])
        mv = sb("mv", [P, 2, 2])
        veps = sb("veps", [P, 2, 1])
        rstd = sb("rstd", [P, 2, 1])
        stat4 = sb("stat4", [P, TB, 6])
        mv4 = sb("mv4", [P, TB, 2])
        veps4 = sb("veps4", [P, TB])
        rstd4 = sb("rstd4", [P, TB])
        topf = sb("topf", [P, TB, TOP])
        dl = sb("dl", [P, TB])
        ex = sb("ex", [P, TB])
        den = sb("den", [P, TB])
        cho = sb("cho", [P, NT, NE], F16)
        slotf = sb("slotf", [P, TOP, TB])
        slots = sb("slots", [P, TOP, NT], U32)
        recs = sb("recs", [P, NT, TOP, 2], U32)
        ntile = sb("ntile", [P, NE])
        icum = sb("icum", [P, NE])
        skip = sb("skip", [P, NE])


        def inside(buf, at, shape, dt=F32):
            n = int(np.prod(shape[1:]))
            v = buf[:].rearrange("p a b -> p (a b)")[:, at:at + n].bitcast(dt)
            names = " ".join("abc"[:len(shape) - 1])
            return v.rearrange(f"p ({names}) -> p {names}", **{k: d for k, d in zip("abc", shape[1:])})

        fill = inside(qst, 0, [P, LISTS, 2], U32)
        lg = inside(u, 0, [P, TB, NE])
        top = inside(u, 32, [P, TB, 8])
        topi = inside(u, 64, [P, TB, 8], U32)
        oh = inside(u, 96, [P, TOP, TB, NE])
        slot = inside(u, 160, [P, TB, NE])
        prod = inside(u, 192, [P, TB, NE])
        jump = inside(u, 224, [P, NJ, NE - 1])
        used = inside(nrm, 0, [P, NE, NT])
        upto = inside(nrm, 128, [P, NE, NE])
        past = inside(nrm, 192, [P, NJ, NE - 1])
        tabf = inside(qst, 0, [P, 2, NJ])
        tab = inside(qst, 2 * NJ, [P, 2, NJ], U32)
        rec = inside(qst, 4 * NJ, [P, NJ, 2], U32)

        ps = [ctx.enter_context(nc.psum_tensor(f"ps{n}", [P, CH], F32)) for n in range(8)]
        psT = ps[4:6]
        psO = ps[6:8]

        names = """vec_in b1_in x_in0 x_in1 consts fill_made stage_in0 stage_in1 st_hi st_lo
            l0_stat l0_agg l0_var l0_rstd l0_nrm l0_vhi l0_vlo l0_tr l0_hi l0_lo
            s_scores s_cmax s_nmax s_bias s_exp s_tr s_hi s_lo s_pv s_rsum s_rinv s_u s_stat s_agg s_var
            s_rstd s_nrm s_gam s_y
            c_scores c_cmax c_nmax c_bias c_exp c_tr c_hi c_lo c_pv c_rsum c_rinv c_u c_stat c_agg c_var
            c_rstd c_nrm c_gam c_y c_qst c_qtr c_qhi c_qlo
            f_ytr f_yhi f_ylo f_up f_relu f_hi f_lo f_down f_xb
            n_yb n_u n_stat n_agg n_var n_rstd n_nrm n_gam n_x1 x2_in0 x2_in1
            m_stat m_agg m_var m_rstd m_h m_hhi m_hlo h_tr h_cp r_logit r_dl r_exp r_cho r_rank r_slot r_rec
            h_out x1_out fill_out rec_out r_count r_tab chain
            rec_in0 rec_in1 rec_in2 rec_in3 e_x0 e_x1 e_xtr e_xcp e_up e_sil e_act e_tr e_ahi e_alo e_down e_y
            e_add""".split()
        sm = {n: sem(n) for n in names}

        def wide(n, a=None):
            return (lambda q: stage[:, q, :n]) if a is None else \
                   (lambda q: stage[:, q, :n].rearrange("p (a n) -> p a n", a=a))

        pieces = []
        for t in range(0, NZ - 1, 2):
            pieces.append((z[t * P:(t + 2) * P, :].rearrange("(a p) d -> p a d", p=P), wide(2 * D, 2),
                           zs[:, 0, t:t + 2, :], zs[:, 1, t:t + 2, :], 1.0))
        pieces.append((z[(NZ - 1) * P:L, :], lambda q: stage[:ZR, q, :D], zs[:ZR, 0, NZ - 1, :],
                       zs[:ZR, 1, NZ - 1, :], 1.0))
        for k in range(KD):
            for a, b in ((0, L // 2), (L // 2, L)):
                pieces.append((zT[k * P:(k + 1) * P, a:b], wide(b - a), zTs[:, 0, k, a:b], zTs[:, 1, k, a:b], 1.0))
        for k in range(KD):
            for a in range(0, DFF, CH):
                pieces.append((w1[k * P:(k + 1) * P, a:a + CH], wide(CH), w1s[:, 0, k, a:a + CH],
                               w1s[:, 1, k, a:a + CH], WS))
        for k in range(0, KF, 2):
            pieces.append((w2[k * P:(k + 2) * P, :].rearrange("(a p) d -> p a d", p=P), wide(2 * D, 2),
                           w2s[:, 0, k:k + 2, :], w2s[:, 1, k:k + 2, :], WS))
        pieces.append((wgT.rearrange("(k p) e -> p k e", p=P), wide(KD * NE, KD), wgs[:, 0], wgs[:, 1], WS))

        def expert_piece(n):
            return (we[n, :, :] if isinstance(n, int) else we[bass.ds(n, 1), :, :].rearrange("a p c -> p (a c)"),
                    wide(CH), ew[:, n, 0, :], ew[:, n, 1, :], WS)

        N_SELF = 2 * NT
        first = 2 * NP
        for n in range(first, first + N_SELF - len(pieces)):
            pieces.append(expert_piece(n))
        second = n + 1
        assert first >= FREE0 and second == 4 * NP
        LAST = 2 * NP - 1
        assert second - 1 + LAST < FREE1
        rest = list(range(second + LAST, NE * NP))

        def wait(eng, name, n):
            eng.wait_ge(sm[name], n)

        def split_load(sp, piece, g, q):
            sp.wait_ge(sm["st_lo"], g - 1) if not (isinstance(g, int) and g < 2) else None
            sp.dma_start(piece[1](q), piece[0]).then_inc(sm[f"stage_in{q}"], 16)

        def split_hi(act_, piece, g, q):
            act_.wait_ge(sm[f"stage_in{q}"], 8 * (g - q) + 16)
            nc.scalar.activation(piece[2], piece[1](q), ACT.Copy, scale=piece[4]).then_inc(sm["st_hi"], 1)

        def split_lo(dve, piece, g, q):
            dve.wait_ge(sm["st_hi"], g + 1)
            nc.vector.scalar_tensor_tensor(piece[3], piece[1](q), piece[4], piece[2], ALU.mult,
                                           ALU.subtract).then_inc(sm["st_lo"], 1)

        def split_cross(fn, eng, s):
            if isinstance(s, int) and s > LAST:
                return
            if isinstance(s, int) and s == 0:
                fn(eng, expert_piece(0), N_SELF, 0)
                return
            fn(eng, expert_piece(s), 2 * s + (N_SELF - 1), 1)
            fn(eng, expert_piece(s + (second - 1)), 2 * s + N_SELF, 0)

        G_FF = N_SELF + 1 + 2 * LAST
        per = -(-len(rest) // NB)

        def split_ff(fn, eng, j, some=None):
            for m, n in enumerate(rest[j * per:(j + 1) * per]):
                g = G_FF + j * per + m
                if some is None or m in some:
                    fn(eng, expert_piece(n), g, g % 2)

        def bridge_dve():
            nc.vector.memset(bridge[:, 0:1], 0.0)

        def bridge_pool(col):
            nc.gpsimd.tensor_tensor(bridge[:, col:col + 1], expo[:, 0:1], expo[:, 0:1], ALU.mult)

        def chunk_of(i):
            return -(-(i + 1) // 4)

        S_CH = [0]
        for i in range(NT):
            S_CH.append(S_CH[-1] + chunk_of(i))
        C_CH = -(-L // CH)
        CW = [CH] * (C_CH - 1) + [L - CH * (C_CH - 1)]
        L0_AT = {0: 1, 2: 2, 4: 3}
        LOOP = (2, NT - 4)

        block = ctx.enter_context(nc.Block())

        def store_x1(sp, j):
            wait(sp, "n_x1", j + 1)
            sp.dma_start(out[j * TB * P:(j + 1) * TB * P, :].rearrange("(m p) d -> p m d", p=P),
                         y[:, j * TB:(j + 1) * TB, :]).then_inc(sm["x1_out"], 16)

        def store_h(sp, j):
            wait(sp, "m_hlo", j + 1)
            sp.dma_start(hrow[j * TB * P:(j + 1) * TB * P, :].rearrange("(m p) c -> p m c", p=P),
                         hs.rearrange("p m a d -> p m (a d)")).then_inc(sm["h_out"], 16)

        @block.sync
        def _(sp):
            def load_x(b, name):
                sp.dma_start(xin[:, b % 2], x[b * TB * P:(b + 1) * TB * P, :].rearrange("(m p) d -> p m d", p=P)
                             ).then_inc(sm[name + str(b % 2)], 16)

            load_x(0, "x_in")
            load_x(1, "x_in")
            split_load(sp, pieces[0], 0, 0)
            split_load(sp, pieces[1], 1, 1)
            sp.dma_start(vec[:].rearrange("p a d -> p (a d)"), rows[:5 * D].partition_broadcast(P)).then_inc(sm["vec_in"], 16)
            sp.dma_start(b1c[:], b1).then_inc(sm["b1_in"], 16)
            wait(sp, "fill_made", 3)
            sp.dma_start(lists.rearrange("(p r) c -> p (r c)", p=P), fill.rearrange("p r c -> p (r c)")
                         ).then_inc(sm["fill_out"], 16)
            sp.dma_start(hrow[S:S + P, :], zero).then_inc(sm["fill_out"], 16)
            sp.dma_start(out[S:S + P, :], zero.bitcast(F32)).then_inc(sm["fill_out"], 16)
            for b in (2, 3):
                wait(sp, "l0_nrm", TB * (b - 1))
                load_x(b, "x_in")
            for g in range(2, N_SELF):
                split_load(sp, pieces[g], g, g % 2)
            split_cross(split_load, sp, 0)
            split_cross(split_load, sp, 1)
            wait(sp, "s_y", NT)
            sp.dma_start(vec[:, 0:2, :].rearrange("p a d -> p (a d)"), rows[5 * D:].partition_broadcast(P)
                         ).then_inc(sm["vec_in"], 16)
            for b in range(2):
                wait(sp, "l0_nrm", TB * (b + 3))
                load_x(b, "x2_in")
            with sp.Fori(LOOP[0], LOOP[1] - 1, 2) as i:
                split_cross(split_load, sp, i)
                split_cross(split_load, sp, i + 1)
            for s in range(LOOP[1], NT):
                split_cross(split_load, sp, s)
            for j in range(NB):
                split_ff(split_load, sp, j)
                if j:
                    store_x1(sp, j - 1)
                    if j + 1 < NB:
                        load_x(j + 1, "x2_in")
                    store_h(sp, j - 1)
            store_x1(sp, NB - 1)
            store_h(sp, NB - 1)
            wait(sp, "r_tab", 1)
            wait(sp, "rec_out", 16 * TOP * NT)
            for n in range(4):
                at = sp.value_load(tab[0:1, 1, n:n + 1], min_val=0, max_val=LISTS - 1)
                sp.dma_start(rec[:, n, :], lists[bass.ds(at * P, P), :]).then_inc(sm[f"rec_in{n}"], 16)
            with sp.Fori(4, NJ - 3, 4) as n:
                for q in range(4):
                    sp.wait_ge(sm[f"rec_in{q}"], 4 * n)
                    at = sp.value_load(tab[0:1, 1, bass.ds(n + q, 1)], min_val=0, max_val=LISTS - 1)
                    sp.dma_start(rec[:, n + q, :], lists[bass.ds(at * P, P), :]).then_inc(sm[f"rec_in{q}"], 16)
            wait(sp, "e_add", 16 * NJ)

        @block.gpsimd
        def _(pool):
            g = nc.gpsimd
            inc = lambda r: r.then_inc(sm["consts"], 1)
            inc(g.memset(ident[:], 0.0))
            inc(g.memset(ident16[:], 0.0))
            inc(g.memset(mask[:], 0.0))
            inc(g.memset(expo[:], -0.5))
            inc(g.memset(ones[:], 1.0))
            inc(g.memset(tri[:], 1.0))
            wait(pool, "consts", 6)
            for t in (ident, ident16):
                inc(g.affine_select(out=t[:], in_=t[:], compare_op=ALU.not_equal, fill=1.0, base=0,
                                    pattern=[[-1, P]], channel_multiplier=1))
            inc(g.affine_select(out=mask[:], in_=mask[:], compare_op=ALU.is_ge, fill=MASKED, base=0,
                                pattern=[[-1, P]], channel_multiplier=1))

            def l0_rstd(b):
                wait(pool, "l0_var", b + 1)
                g.tensor_tensor(rstd4[:], veps4[:], expo[:], ALU.pow).then_inc(sm["l0_rstd"], 1)

            def l0_vlo(b):
                wait(pool, "l0_vhi", b + 1)
                g.tensor_tensor(yv[:, 1, b * TB:(b + 1) * TB, :], y[:, b * TB:(b + 1) * TB, :],
                                yv[:, 0, b * TB:(b + 1) * TB, :], ALU.subtract).then_inc(sm["l0_vlo"], 1)

            l0_rstd(0)
            l0_vlo(0)
            iota = lambda o, pat, base=0, mult=0: inc(g.iota(o, pattern=pat, base=base, channel_multiplier=mult,
                                                             allow_small_or_imprecise_dtypes=True))
            inc(g.affine_select(out=tri[:], in_=tri[:], compare_op=ALU.is_gt, fill=0.0, base=0,
                                pattern=[[1, P]], channel_multiplier=-1))
            iota(iota8[:], [[1, NE]])
            iota(ebase[:], [[BL * P, NE]])
            iota(cuts[:], [[P, NT]])
            iota(jot[:], [[1, NJ]])
            iota(recs[:].rearrange("p t c w -> p t (c w)"), [[P, NT], [0, 2 * TOP]], 0, 1)
            iota(fill, [[1, LISTS], [0, 2]], 0, LISTS)
            inc(g.memset(tri8[:], 1.0))
            wait(pool, "consts", 17)
            inc(g.affine_select(out=tri8[:], in_=tri8[:], compare_op=ALU.is_ge, fill=0.0, base=0,
                                pattern=[[1, NE], [-1, NE]], channel_multiplier=0))

            def ln_rstd(pre, i, q):
                pool.wait_ge(sm[pre + "var"], i + 1)
                g.tensor_tensor(rstd[:, q, :], veps[:, q, :], expo[:, 0:1], ALU.pow).then_inc(sm[pre + "rstd"], 1)

            def ln_affine(pre, i, q, row):
                pool.wait_ge(sm[pre + "nrm"], i + 1)
                g.tensor_tensor(nrm[:, q, :], nrm[:, q, :], vec[:, row, :], ALU.mult).then_inc(sm[pre + "gam"], 1)
                pool.wait_ge(sm[pre + "gam"], i + 1)
                if not isinstance(i, int):
                    bridge_pool(1)
                g.tensor_tensor(y[:, i, :], nrm[:, q, :], vec[:, row + 1, :], ALU.add).then_inc(sm[pre + "y"], 1)

            wait(pool, "vec_in", 16)
            for i in range(NT + 1):
                if i:
                    ln_rstd("s_", i - 1, (i - 1) % 2)
                    ln_affine("s_", i - 1, (i - 1) % 2, 0)
                if i in L0_AT:
                    l0_rstd(L0_AT[i])
                    l0_vlo(L0_AT[i])

            def q_stage(t, q):
                if not (isinstance(t, int) and t < 2):
                    pool.wait_ge(sm["c_qtr"], t - 1)
                    bridge_pool(2)
                g.tensor_copy(qst[:, q, :], y[:, t, :]).then_inc(sm["c_qst"], 1)

            wait(pool, "s_y", NT)
            q_stage(0, 0)
            q_stage(1, 1)

            def c_step(i, q):
                if not isinstance(i, int) or i + 2 < NT:
                    q_stage(i + 2, q)
                ln_rstd("c_", i, q)
                ln_affine("c_", i, q, 2)

            for i in range(LOOP[0]):
                c_step(i, i % 2)
            with pool.Fori(LOOP[0], LOOP[1] - 1, 2) as i:
                c_step(i, 0)
                c_step(i + 1, 1)
            for i in range(LOOP[1], NT):
                c_step(i, i % 2)
            wait(pool, "c_y", NT)

            def bc(row, n=TB):
                return vec[:, row, :].unsqueeze(1).broadcast_to([P, n, D])

            def blk(j):
                return y[:, j * TB:(j + 1) * TB, :]

            def x_beta(j):
                wait(pool, f"x2_in{j % 2}", 16 * (j // 2 + 1))
                g.tensor_tensor(xin[:, j % 2], xin[:, j % 2], bc(1), ALU.add).then_inc(sm["f_xb"], 1)

            def y_b2(j):
                wait(pool, "f_ytr", j + 1)
                g.tensor_tensor(blk(j), blk(j), bc(4), ALU.add).then_inc(sm["n_yb"], 1)

            def rstd_of(pre, j):
                wait(pool, pre + "var", j + 1)
                g.tensor_tensor(rstd4[:], veps4[:], expo[:], ALU.pow).then_inc(sm[pre + "rstd"], 1)

            def x1(j):
                wait(pool, "n_nrm", TB * (j + 1))
                g.tensor_tensor(n4, n4, bc(0), ALU.mult).then_inc(sm["n_gam"], 1)
                wait(pool, "n_gam", j + 1)
                wait(pool, "f_xb", j + 1)
                g.tensor_tensor(blk(j), n4, xin[:, j % 2], ALU.add).then_inc(sm["n_x1"], 1)

            def scatter(j, ms):
                wait(pool, "r_slot", j + 1)
                wait(pool, "r_rec", TOP * (j + 1))
                for m in ms:
                    for c in range(TOP):
                        t = j * TB + m
                        g.indirect_dma_start(lists, bass.IndirectOffsetOnAxis(slots[:, c, t:t + 1], 0),
                                             recs[:, t, c, :], None).then_inc(sm["rec_out"], 16)

            wait(pool, "fill_out", 48)
            wait(pool, "vec_in", 32)
            x_beta(0)
            x_beta(1)
            y_b2(0)
            for j in range(NB):
                if j:
                    x1(j - 1)
                    rstd_of("m_", j - 1)
                    if j + 1 < NB:
                        x_beta(j + 1)
                if j > 1:
                    scatter(j - 2, (2, 3))
                if j + 1 < NB:
                    y_b2(j + 1)
                if j:
                    scatter(j - 1, (0, 1))
                rstd_of("n_", j)
            x1(NB - 1)
            rstd_of("m_", NB - 1)
            scatter(NB - 2, (2, 3))
            scatter(NB - 1, range(TB))

            def gather(n):
                if n >= 2:
                    wait(pool, "e_xtr", n - 1)
                wait(pool, f"rec_in{n % 4}", 16 * (n // 4 + 1))
                g.indirect_dma_start(xg[:, n % 2, :], None, hrow,
                                     bass.IndirectOffsetOnAxis(rec[:, n, 0:1], 0)).then_inc(sm[f"e_x{n % 2}"], 16)

            def add(n):
                wait(pool, "e_y", n + 1)
                if n:
                    wait(pool, "e_add", 16 * n)
                g.indirect_dma_start(out, bass.IndirectOffsetOnAxis(rec[:, n, 0:1], 0), ys[:, n % 2, :], None,
                                     compute_op=ALU.add).then_inc(sm["e_add"], 16)

            wait(pool, "h_out", 16 * NB)
            wait(pool, "x1_out", 16 * NB)
            gather(0)
            gather(1)
            gather(2)
            for n in range(NJ):
                if n + 3 < NJ:
                    gather(n + 3)
                if n:
                    add(n - 1)
            add(NJ - 1)

        @block.scalar
        def _(act_):
            a = nc.scalar

            def copy(o, i):
                return a.activation(o, i, ACT.Copy)

            def l0_his(b):
                wait(act_, "l0_nrm", TB * (b + 1))
                copy(yv[:, 0, b * TB:(b + 1) * TB, :], y[:, b * TB:(b + 1) * TB, :]).then_inc(sm["l0_vhi"], 1)
                wait(act_, "l0_tr", b + 1)
                for k in range(KD):
                    copy(yT[:, 0, k, b * TB:(b + 1) * TB, :],
                         ps[2 + k][:].rearrange("p (m t) -> p m t", m=TB)).then_inc(sm["l0_hi"], 1)

            def exps(pre, q, count, c, w):
                act_.wait_ge(sm[pre + "bias"], count)
                a.activation(prob[:, q, c * CH:c * CH + w], ps[c][:, :w], ACT.Exp, bias=nbias[:, q, :], scale=SM,
                             accum_out=esum[:, q, c:c + 1]).then_inc(sm[pre + "exp"], 1)

            grp = [0]

            def s_his(i, g):
                n = min(4, i + 1 - 4 * g)
                grp[0] += 1
                wait(act_, "s_tr", grp[0])
                copy(probT[:, i % 2, 0, 4 * g:4 * g + n, :],
                     psT[(grp[0] - 1) % 2][:, :n * P].rearrange("p (k t) -> p k t", k=n)).then_inc(sm["s_hi"], 1)

            def s_exps(i, c):
                exps("s_", i % 2, i + 1, c, min(CH, (i + 1) * P - c * CH))

            l0_his(0)
            s_exps(0, 0)
            for i in range(NT):
                ng = chunk_of(i)
                nch = chunk_of(i + 1) if i + 1 < NT else 0
                for g in range(min(2, ng)):
                    s_his(i, g)
                for c in range(min(2, nch)):
                    s_exps(i + 1, c)
                if ng > 2:
                    s_his(i, 2)
                for c in range(2, nch):
                    s_exps(i + 1, c)
                if ng > 3:
                    s_his(i, 3)
                if i in L0_AT:
                    l0_his(L0_AT[i])
                for n in (2 * i, 2 * i + 1):
                    split_hi(act_, pieces[n], n, n % 2)

            def q_hi(t, q, k):
                act_.wait_ge(sm["c_qtr"], t + 1)
                copy(qT[:, q, 0, :, :], psT[k][:, P:P + D].rearrange("p (k t) -> p k t", k=KD)).then_inc(sm["c_qhi"], 1)

            def c_his(i, q, g, nxt2=False):
                act_.wait_ge(sm["c_tr"], 4 * i + g + 1)
                if nxt2:
                    act_.wait_ge(sm["c_qtr"], i + 3)
                n = 4 if g < 3 else 1
                r = P if g < 3 else ZR
                copy(probT[:r, q, 0, 4 * g:4 * g + n, :],
                     psT[g % 2][:r, :n * P].rearrange("p (k t) -> p k t", k=n)).then_inc(sm["c_hi"], 1)

            def c_exps(t, q, c):
                exps("c_", q, t + 1, c, CW[c])

            wait(act_, "fill_out", 48)
            q_hi(0, 0, 0)
            q_hi(1, 1, 1)
            for c in range(C_CH):
                c_exps(0, 0, c)

            def c_step(i, q, nxt=True, nxt2=True):
                c_his(i, q, 0)
                c_his(i, q, 1)
                if nxt:
                    c_exps(i + 1, 1 - q, 0)
                    c_exps(i + 1, 1 - q, 1)
                c_his(i, q, 2)
                if nxt:
                    c_exps(i + 1, 1 - q, 2)
                    c_exps(i + 1, 1 - q, 3)
                c_his(i, q, 3, nxt2)
                if nxt2:
                    q_hi(i + 2, q, 1)
                split_cross(split_hi, act_, i)

            for i in range(LOOP[0]):
                c_step(i, i % 2)
            with act_.Fori(LOOP[0], LOOP[1] - 1, 2) as i:
                c_step(i, 0)
                c_step(i + 1, 1)
            for i in range(LOOP[1], NT):
                c_step(i, i % 2, i + 1 < NT, i + 2 < NT)

            def y_hi(j):
                wait(act_, "f_ytr", j + 1)
                for k in range(KD):
                    copy(ybT[:, 0, k, :], psT[k][:]).then_inc(sm["f_yhi"], 1)

            def relu(j, f):
                wait(act_, "f_up", j * KF + f + 1)
                if f >= 2:
                    wait(act_, "f_lo", j * KF + f - 1)
                a.activation(hid[:, f % 2, :], ps[f % 2][:], ACT.Relu, bias=b1c[:, f:f + 1],
                             scale=1.0 / WS).then_inc(sm["f_relu"], 1)
                wait(act_, "f_relu", j * KF + f + 1)
                copy(hidT[:, 0, f, :], hid[:, f % 2, :]).then_inc(sm["f_hi"], 1)

            def h_hi(j):
                wait(act_, "m_h", TB * (j + 1))
                if j:
                    wait(act_, "h_out", 16 * j)
                copy(hs[:, :, 0, :], h4).then_inc(sm["m_hhi"], 1)

            def h_copy(j):
                wait(act_, "h_tr", j + 1)
                for n in range(2):
                    copy(hT[:, 2 * n:2 * n + 2].rearrange("p m a k c -> p (m a k c)"),
                         ps[2 + n][:].bitcast(F16)).then_inc(sm["h_cp"], 1)

            def gates(j):
                wait(act_, "r_dl", j + 1)
                a.activation(ex[:], dl[:], ACT.Exp).then_inc(sm["r_exp"], 1)

            wait(act_, "b1_in", 16)
            y_hi(0)
            for j in range(NB):
                for f in range(KF):
                    relu(j, f)
                    if f % 2 == 0:
                        split_ff(split_hi, act_, j, (f // 2,))
                if j:
                    h_hi(j - 1)
                    h_copy(j - 1)
                if j + 1 < NB:
                    y_hi(j + 1)
                if j:
                    gates(j - 1)
            h_hi(NB - 1)
            h_copy(NB - 1)
            gates(NB - 1)

            def x_copy(n, q):
                act_.wait_ge(sm["e_xtr"], n + 1)
                copy(xT[:, q, :, :].rearrange("p b c -> p (b c)"), psO[q][:, D:].bitcast(F16)).then_inc(sm["e_xcp"], 1)

            def silu(n, q):
                act_.wait_ge(sm["e_up"], n + 1)
                a.activation(sil[:, q, :], ps[2 * q][:], ACT.Silu, scale=1.0 / WS).then_inc(sm["e_sil"], 1)

            def act_hi(n, q):
                act_.wait_ge(sm["e_tr"], n + 1)
                copy(actT[:, q, 0, :, :].rearrange("p k t -> p (k t)"), psT[q][:]).then_inc(sm["e_ahi"], 1)

            def e_step(n, q, nxt=True):
                silu(n, q)
                act_hi(n - 1, 1 - q)
                if nxt:
                    x_copy(n + 1, 1 - q)

            x_copy(0, 0)
            silu(0, 0)
            x_copy(1, 1)
            e_step(1, 1)
            with act_.Fori(2, NJ - 3, 2) as n:
                e_step(n, 0)
                e_step(n + 1, 1)
            e_step(NJ - 2, 0)
            e_step(NJ - 1, 1, False)
            act_hi(NJ - 1, 1)

        @block.tensor
        def _(pe):
            t = nc.tensor

            def mm3(o, lhs, rhs, first, last):
                for n, (a, b) in enumerate(PARTS):
                    r = t.matmul(o, lhs(a), rhs(b), start=first and n == 0, stop=last and n == 2)
                return r

            def l0_trans(b):
                wait(pe, "l0_nrm", TB * (b + 1))
                if b:
                    wait(pe, "l0_lo", KD * b)
                for k in range(KD):
                    for m in range(TB):
                        r = t.transpose(ps[2 + k][:, m * P:(m + 1) * P], y[:, b * TB + m, k * P:(k + 1) * P], ident[:])
                r.then_inc(sm["l0_tr"], 1)

            wait(pe, "consts", 9)
            l0_trans(0)

            grp = [0]

            def s_scores(i):
                n = chunk_of(i)
                wait(pe, "l0_lo", KD * (i // TB + 1))
                for c in range(n):
                    w = min(CH, (i + 1) * P - c * CH)
                    prev = [j for j in range(i) if chunk_of(j) > c]
                    if prev:
                        wait(pe, "s_exp", S_CH[prev[-1]] + c + 1)
                    o = ps[c][:, :w]
                    diag = c == n - 1
                    for k in range(KD):
                        r = mm3(o, lambda a: yT[:, a, k, i, :],
                                lambda b: yT[:, b, k, 4 * c:4 * c + w // P, :],
                                k == 0, k == KD - 1 and not diag)
                    if diag:
                        r = t.matmul(ps[c][:, w - P:w], ident16[:], mask[:], start=False, stop=True)
                    r.then_inc(sm["s_scores"], 1)

            def s_trans(i, g):
                grp[0] += 1
                k = grp[0] - 1
                if k >= 2:
                    wait(pe, "s_lo", k - 1)
                if g == 0:
                    wait(pe, "s_exp", S_CH[i + 1])
                n = min(4, i + 1 - 4 * g)
                for m in range(n):
                    r = t.transpose(psT[k % 2][:, m * P:(m + 1) * P],
                                    prob[:, i % 2, (4 * g + m) * P:(4 * g + m + 1) * P], ident[:])
                r.then_inc(sm["s_tr"], 1)

            def s_pv(i, g):
                wait(pe, "s_lo", S_CH[i] + g + 1)
                if g == 0:
                    wait(pe, "l0_vlo", i // TB + 1)
                    if i >= 2:
                        wait(pe, "s_u", i - 1)
                for m in range(4 * g, min(4 * g + 4, i + 1)):
                    r = mm3(psO[i % 2][:, :D], lambda a: probT[:, i % 2, a, m, :], lambda b: yv[:, b, m, :],
                            m == 0, m == i)
                if 4 * g + 4 >= i + 1:
                    r.then_inc(sm["s_pv"], 1)

            s_scores(0)
            for i in range(NT):
                ng = chunk_of(i)
                for g in range(min(2, ng)):
                    s_trans(i, g)
                if i + 1 < NT:
                    s_scores(i + 1)
                for g in range(ng):
                    s_pv(i, g)
                    if g + 2 < ng:
                        s_trans(i, g + 2)
                if i in L0_AT:
                    l0_trans(L0_AT[i])

            def q_trans(i, q, k):
                pe.wait_ge(sm["c_qst"], i + 1)
                for m in range(KD):
                    r = t.transpose(psT[k][:, (m + 1) * P:(m + 2) * P], qst[:, q, m * P:(m + 1) * P], ident[:])
                r.then_inc(sm["c_qtr"], 1)

            def c_scores(i, q, first=False):
                pe.wait_ge(sm["c_qlo"], i + 1)
                for c in range(C_CH):
                    if not first:
                        pe.wait_ge(sm["c_exp"], 4 * i + (c - 3))
                    w = CW[c]
                    for k in range(KD):
                        r = mm3(ps[c][:, :w], lambda a: qT[:, q, a, k, :],
                                lambda b: zTs[:, b, k, c * CH:c * CH + w], k == 0, k == KD - 1)
                    r.then_inc(sm["c_scores"], 1)

            def c_trans(i, q, g):
                if g >= 2 or not (isinstance(i, int) and i == 0):
                    pe.wait_ge(sm["c_lo"], 4 * i + g - 1)
                if g == 1 and not (isinstance(i, int) and i == 0):
                    pe.wait_ge(sm["c_qlo"], min(i + 2, NT) if isinstance(i, int) else i + 2)
                if g == 0:
                    pe.wait_ge(sm["c_exp"], 4 * i + 4)
                for m in range(4 * g, min(4 * g + 4, NZ)):
                    r_ = P if m < NZ - 1 else ZR
                    r = t.transpose(psT[g % 2][:r_, (m % 4) * P:(m % 4 + 1) * P],
                                    prob[:, q, m * P:m * P + r_], ident[:])
                r.then_inc(sm["c_tr"], 1)

            def c_pv(i, q, g):
                pe.wait_ge(sm["c_lo"], 4 * i + g + 1)
                if g == 0 and not (isinstance(i, int) and i < 2):
                    pe.wait_ge(sm["c_u"], i - 1)
                for m in range(4 * g, min(4 * g + 4, NZ)):
                    r_ = P if m < NZ - 1 else ZR
                    r = mm3(psO[q][:, :D], lambda a: probT[:r_, q, a, m, :], lambda b: zs[:r_, b, m, :],
                            m == 0, m == NZ - 1)
                if g == 3:
                    r.then_inc(sm["c_pv"], 1)

            wait(pe, "s_lo", grp[0])
            wait(pe, "s_u", NT)
            q_trans(0, 0, 0)
            q_trans(1, 1, 1)
            wait(pe, "st_lo", 11)
            c_scores(0, 0, True)

            def c_step(i, q, nxt=True, nxt2=True):
                c_trans(i, q, 0)
                c_trans(i, q, 1)
                if nxt:
                    c_scores(i + 1, 1 - q)
                c_pv(i, q, 0)
                c_trans(i, q, 2)
                c_pv(i, q, 1)
                c_trans(i, q, 3)
                if nxt2:
                    q_trans(i + 2, q, 1)
                c_pv(i, q, 2)
                c_pv(i, q, 3)

            for i in range(LOOP[0]):
                c_step(i, i % 2)
            with pe.Fori(LOOP[0], LOOP[1] - 1, 2) as i:
                c_step(i, 0)
                c_step(i + 1, 1)
            for i in range(LOOP[1], NT):
                c_step(i, i % 2, i + 1 < NT, i + 2 < NT)

            wait(pe, "c_lo", 4 * NT)
            wait(pe, "c_exp", 4 * NT)
            wait(pe, "c_u", NT)
            wait(pe, "st_lo", N_SELF)

            def y_trans(j):
                wait(pe, "c_y", TB * (j + 1))
                if j:
                    wait(pe, "f_ylo", KD * j)
                for k in range(KD):
                    for m in range(TB):
                        r = t.transpose(psT[k][:, m * P:(m + 1) * P], y[:, j * TB + m, k * P:(k + 1) * P], ident[:])
                r.then_inc(sm["f_ytr"], 1)

            def ups(j):
                wait(pe, "f_ylo", KD * (j + 1))
                for f in range(KF):
                    if KF * j + f >= 2:
                        wait(pe, "f_relu", KF * j + f - 1)
                    for k in range(KD):
                        r = mm3(ps[f % 2][:], lambda a: w1s[:, a, k, f * P:(f + 1) * P], lambda b: ybT[:, b, k, :],
                                k == 0, k == KD - 1)
                    r.then_inc(sm["f_up"], 1)

            def down(j, m):
                if m == 0:
                    wait(pe, "f_lo", KF * (j + 1))
                n = j * TB + m
                if n >= 2:
                    wait(pe, "n_u", n - 1)
                for f in range(KF):
                    r = mm3(psO[m % 2][:, :D], lambda a: hidT[:, a, f, m * P:(m + 1) * P], lambda b: w2s[:, b, f, :],
                            f == 0, f == KF - 1)
                r.then_inc(sm["f_down"], 1)

            def h_trans(j):
                wait(pe, "m_hlo", j + 1)
                if j:
                    wait(pe, "r_slot", j)
                for m in range(TB):
                    for a in range(2):
                        for k in range(KD):
                            c = ((m % 2) * 2 * KD + a * KD + k) * P
                            r = t.transpose(ps[2 + m // 2][:].bitcast(F16)[:, c:c + P],
                                            hs[:, m, a, k * P:(k + 1) * P], ident16[:])
                r.then_inc(sm["h_tr"], 1)

            def logits(j):
                wait(pe, "h_cp", 2 * (j + 1))
                for m in range(TB):
                    for k in range(KD):
                        r = mm3(ps[2][:, m * NE:(m + 1) * NE], lambda a: hT[:, m, a, k, :], lambda b: wgs[:, b, k, :],
                                k == 0, k == KD - 1)
                r.then_inc(sm["r_logit"], 1)

            def ranks(j):
                wait(pe, "consts", 18)
                wait(pe, "r_cho", j + 1)
                for m in range(TB):
                    n = j * TB + m
                    o = ps[3][:, m * NE:(m + 1) * NE]
                    r = t.matmul(o, tri[:], cho[:, n, :], start=True, stop=n == 0)
                    for b in range(n):
                        r = t.matmul(o, ones[:], cho[:, b, :], start=False, stop=b == n - 1)
                r.then_inc(sm["r_rank"], 1)

            y_trans(0)
            for j in range(NB):
                ups(j)
                if j:
                    h_trans(j - 1)
                if j + 1 < NB:
                    y_trans(j + 1)
                if j:
                    logits(j - 1)
                down(j, 0)
                down(j, 1)
                if j:
                    ranks(j - 1)
                down(j, 2)
                down(j, 3)
            h_trans(NB - 1)
            logits(NB - 1)
            ranks(NB - 1)
            for n in range(NT):
                r = t.matmul(ps[2][:, CH - NE:], ones[:], cho[:, n, :], start=n == 0, stop=n == NT - 1)
            r.then_inc(sm["r_count"], 1)

            def x_trans(n, q):
                pe.wait_ge(sm[f"e_x{q}"], 8 * (n - q) + 16)
                if not (isinstance(n, int) and n < 4):
                    pe.wait_ge(sm["e_y"], n - 3)
                for b in range(2 * KD):
                    r = t.transpose(psO[q][:, D:].bitcast(F16)[:, b * P:(b + 1) * P], xg[:, q, b * P:(b + 1) * P],
                                    ident16[:])
                r.then_inc(sm["e_xtr"], 1)

            def e_ups(n, q):
                at = pe.value_load(tab[0:1, 0, bass.ds(n, 1)], min_val=0, max_val=(NE - 1) * NP)
                pe.wait_ge(sm["e_xcp"], n + 1)
                if not (isinstance(n, int) and n < 2):
                    pe.wait_ge(sm["e_act"], n - 1)
                for h in range(2):
                    for k in range(KD):
                        r = mm3(ps[2 * q + h][:], lambda a: xT[:, q, a * KD + k, :],
                                lambda b: ew[:, at + (k * 2 + h), b, :], k == 0, k == KD - 1)
                r.then_inc(sm["e_up"], 1)

            def e_trans(n, q):
                pe.wait_ge(sm["e_act"], n + 1)
                if not (isinstance(n, int) and n < 2):
                    pe.wait_ge(sm["e_alo"], n - 1)
                for k in range(KI):
                    r = t.transpose(psT[q][:, k * P:(k + 1) * P], act[:, q, k * P:(k + 1) * P], ident[:])
                r.then_inc(sm["e_tr"], 1)

            def e_downs(n, q, nxt=2):
                at = pe.value_load(tab[0:1, 0, bass.ds(n, 1)], min_val=0, max_val=(NE - 1) * NP)
                pe.wait_ge(sm["e_alo"], n + 1)
                if nxt:
                    pe.wait_ge(sm["e_xcp"], n + 1 + nxt)
                for k in range(KI):
                    r = mm3(psO[q][:, :D], lambda a: actT[:, q, a, k, :],
                            lambda b: ew[:, at + (2 * KD + k // 2), b, (k % 2) * D:(k % 2 + 1) * D],
                            k == 0, k == KI - 1)
                r.then_inc(sm["e_down"], 1)

            wait(pe, "r_tab", 1)
            wait(pe, "r_slot", NB)
            wait(pe, "n_u", NT)
            wait(pe, "st_lo", G_FF + len(rest))
            x_trans(0, 0)
            e_ups(0, 0)
            x_trans(1, 1)
            e_ups(1, 1)
            e_trans(0, 0)
            x_trans(2, 0)

            def e_step(n, q, nxt=True):
                e_ups(n, q)
                e_trans(n - 1, 1 - q)
                if nxt:
                    x_trans(n + 1, 1 - q)
                e_downs(n - 2, q)

            e_step(2, 0)
            e_step(3, 1)
            with pe.Fori(4, NJ - 3, 2) as n:
                e_step(n, 0)
                e_step(n + 1, 1)
            e_step(NJ - 2, 0)
            e_step(NJ - 1, 1, False)
            e_trans(NJ - 1, 1)
            e_downs(NJ - 2, 0, 0)
            e_downs(NJ - 1, 1, 0)

        @block.vector
        def _(dve):
            v = nc.vector
            links = [0]

            def link(ins):
                links[0] += 1
                ins.then_inc(sm["chain"], 1)
                dve.wait_ge(sm["chain"], links[0])

            def moments(pre, src, q, i):
                v.bn_stats(stat[:, q, :], src).then_inc(sm[pre + "stat"], 1)
                dve.wait_ge(sm[pre + "stat"], i + 1)
                if not isinstance(i, int):
                    bridge_dve()
                v.bn_aggr(mv[:, q, :], stat[:, q, :]).then_inc(sm[pre + "agg"], 1)
                dve.wait_ge(sm[pre + "agg"], i + 1)
                v.tensor_scalar(veps[:, q, :], mv[:, q, 1:2], EPS, None, ALU.add).then_inc(sm[pre + "var"], 1)

            def normalise(pre, src, q, i):
                dve.wait_ge(sm[pre + "rstd"], i + 1)
                v.tensor_scalar(nrm[:, q, :], src, mv[:, q, 0:1], rstd[:, q, :], ALU.subtract,
                                ALU.mult).then_inc(sm[pre + "nrm"], 1)

            def moments4(pre, src, b):
                for m in range(TB):
                    v.bn_stats(stat4[:, m, :], src(m)).then_inc(sm[pre + "stat"], 1)
                wait(dve, pre + "stat", TB * (b + 1))
                aggregate4(pre, b)

            def aggregate4(pre, b):
                for m in range(TB):
                    v.bn_aggr(mv4[:, m, :], stat4[:, m, :]).then_inc(sm[pre + "agg"], 1)
                wait(dve, pre + "agg", TB * (b + 1))
                v.tensor_scalar(veps4[:], mv4[:, :, 1], EPS, None, ALU.add).then_inc(sm[pre + "var"], 1)

            def normalise4(pre, src, dst, b, done):
                wait(dve, pre + "rstd", b + 1)
                for m in range(TB):
                    v.tensor_scalar(dst(m), src(m), mv4[:, m, 0:1], rstd4[:, m:m + 1], ALU.subtract,
                                    ALU.mult).then_inc(sm[done], 1)

            def l0_stats(b):
                wait(dve, f"x_in{b % 2}", 16 * (b // 2 + 1))
                moments4("l0_", lambda m: xin[:, b % 2, m, :], b)

            def l0_norm(b):
                normalise4("l0_", lambda m: xin[:, b % 2, m, :], lambda m: y[:, b * TB + m, :], b, "l0_nrm")

            def l0_los(b):
                for k in range(KD):
                    wait(dve, "l0_hi", KD * b + k + 1)
                    v.tensor_tensor(yT[:, 1, k, b * TB:(b + 1) * TB, :],
                                    ps[2 + k][:].rearrange("p (m t) -> p m t", m=TB),
                                    yT[:, 0, k, b * TB:(b + 1) * TB, :], ALU.subtract).then_inc(sm["l0_lo"], 1)

            l0_stats(0)
            l0_norm(0)
            l0_los(0)

            def maxes(pre, q, c, w, scores):
                dve.wait_ge(sm[pre + "scores"], scores)
                v.tensor_reduce(cmax[:, q, c:c + 1], ps[c][:, :w], X, ALU.max).then_inc(sm[pre + "cmax"], 1)

            def bias(pre, q, n, i, count):
                dve.wait_ge(sm[pre + "cmax"], count)
                v.tensor_reduce(nmax[:, q, :], cmax[:, q, :n], X, ALU.max, negate=True).then_inc(sm[pre + "nmax"], 1)
                dve.wait_ge(sm[pre + "nmax"], i + 1)
                v.tensor_scalar(nbias[:, q, :], nmax[:, q, :], SM, None, ALU.mult).then_inc(sm[pre + "bias"], 1)

            def sums(pre, q, n, i, count):
                dve.wait_ge(sm[pre + "exp"], count)
                v.tensor_reduce(rsum[:, q, :], esum[:, q, :n], X, ALU.add).then_inc(sm[pre + "rsum"], 1)
                dve.wait_ge(sm[pre + "rsum"], i + 1)
                v.reciprocal(rinv[:, q, :], rsum[:, q, :]).then_inc(sm[pre + "rinv"], 1)

            def residual(pre, i, q):
                dve.wait_ge(sm[pre + "rinv"], i + 1)
                dve.wait_ge(sm[pre + "pv"], i + 1)
                v.scalar_tensor_tensor(u[:, q, :], psO[q][:, :D], rinv[:, q, :], y[:, i, :], ALU.mult,
                                       ALU.add).then_inc(sm[pre + "u"], 1)
                dve.wait_ge(sm[pre + "u"], i + 1)
                moments(pre, u[:, q, :], q, i)

            grp = [0]

            def s_los(i, g):
                n = min(4, i + 1 - 4 * g)
                grp[0] += 1
                wait(dve, "s_hi", grp[0])
                k = (grp[0] - 1) % 2
                v.tensor_tensor(probT[:, i % 2, 1, 4 * g:4 * g + n, :],
                                psT[k][:, :n * P].rearrange("p (k t) -> p k t", k=n),
                                probT[:, i % 2, 0, 4 * g:4 * g + n, :], ALU.subtract).then_inc(sm["s_lo"], 1)

            def s_max(i):
                for c in range(chunk_of(i)):
                    maxes("s_", i % 2, c, min(CH, (i + 1) * P - c * CH), S_CH[i] + c + 1)
                bias("s_", i % 2, chunk_of(i), i, S_CH[i + 1])

            def s_norm(i):
                if i >= 2:
                    wait(dve, "s_y", i - 1)
                normalise("s_", u[:, i % 2, :], i % 2, i)

            s_max(0)
            v.memset(zero.bitcast(U32), 0).then_inc(sm["fill_made"], 1)
            wait(dve, "consts", 18)
            v.memset(fill[:, :, 1], 0).then_inc(sm["fill_made"], 1)
            v.tensor_scalar(fill[:, :, 0], fill[:, :, 0], P - 1, S, ALU.bitwise_and,
                            ALU.bitwise_or).then_inc(sm["fill_made"], 1)
            for i in range(NT):
                ng = chunk_of(i)
                for g in range(min(2, ng)):
                    s_los(i, g)
                if i:
                    residual("s_", i - 1, (i - 1) % 2)
                if i + 1 < NT:
                    s_max(i + 1)
                if i:
                    s_norm(i - 1)
                sums("s_", i % 2, ng, i, S_CH[i + 1])
                for g in range(2, ng):
                    s_los(i, g)
                if i in L0_AT:
                    b = L0_AT[i]
                    l0_stats(b)
                    l0_norm(b)
                    l0_los(b)
                for n in (2 * i, 2 * i + 1):
                    split_lo(dve, pieces[n], n, n % 2)
            residual("s_", NT - 1, (NT - 1) % 2)
            s_norm(NT - 1)

            def q_lo(t, q, k):
                dve.wait_ge(sm["c_qhi"], t + 1)
                v.tensor_tensor(qT[:, q, 1, :, :], psT[k][:, P:P + D].rearrange("p (k t) -> p k t", k=KD),
                                qT[:, q, 0, :, :], ALU.subtract).then_inc(sm["c_qlo"], 1)

            def c_los(i, q, g, nxt2=False):
                n = 4 if g < 3 else 1
                r = P if g < 3 else ZR
                dve.wait_ge(sm["c_hi"], 4 * i + g + 1)
                if nxt2:
                    dve.wait_ge(sm["c_qhi"], i + 3)
                v.tensor_tensor(probT[:r, q, 1, 4 * g:4 * g + n, :],
                                psT[g % 2][:r, :n * P].rearrange("p (k t) -> p k t", k=n),
                                probT[:r, q, 0, 4 * g:4 * g + n, :], ALU.subtract).then_inc(sm["c_lo"], 1)

            def c_max(i, q):
                for c in range(C_CH):
                    maxes("c_", q, c, CW[c], 4 * i + c + 1)
                bias("c_", q, C_CH, i, 4 * i + 4)

            def c_norm(i, q):
                if not (isinstance(i, int) and i < 2):
                    dve.wait_ge(sm["c_y"], i - 1)
                normalise("c_", u[:, q, :], q, i)

            def c_step(i, q, nxt=True, nxt2=True):
                c_los(i, q, 0)
                c_los(i, q, 1)
                prev = not (isinstance(i, int) and i == 0)
                if prev:
                    residual("c_", i - 1, 1 - q)
                if nxt:
                    c_max(i + 1, 1 - q)
                if prev:
                    c_norm(i - 1, 1 - q)
                sums("c_", q, C_CH, i, 4 * i + 4)
                c_los(i, q, 2)
                c_los(i, q, 3, nxt2)
                if nxt2:
                    q_lo(i + 2, q, 1)
                split_cross(split_lo, dve, i)

            wait(dve, "s_y", NT)
            q_lo(0, 0, 0)
            q_lo(1, 1, 1)
            c_max(0, 0)
            for i in range(LOOP[0] + 2):
                c_step(i, i % 2)
            with dve.Fori(LOOP[0] + 2, LOOP[1] - 1, 2) as i:
                c_step(i, 0)
                c_step(i + 1, 1)
            for i in range(LOOP[1], NT):
                c_step(i, i % 2, i + 1 < NT, i + 2 < NT)
            residual("c_", NT - 1, 1)
            c_norm(NT - 1, 1)
            wait(dve, "c_y", NT)

            def y_lo(j):
                for k in range(KD):
                    wait(dve, "f_yhi", KD * j + k + 1)
                    v.tensor_tensor(ybT[:, 1, k, :], psT[k][:], ybT[:, 0, k, :], ALU.subtract).then_inc(sm["f_ylo"], 1)

            def hid_lo(j, f):
                wait(dve, "f_hi", KF * j + f + 1)
                v.tensor_tensor(hidT[:, 1, f, :], hid[:, f % 2, :], hidT[:, 0, f, :],
                                ALU.subtract).then_inc(sm["f_lo"], 1)

            def out_tile(j, m):
                n = j * TB + m
                wait(dve, "f_down", n + 1)
                wait(dve, "n_yb", j + 1)
                v.scalar_tensor_tensor(u4[:, m, :], psO[m % 2][:, :D], 1.0 / WS, y[:, n, :], ALU.mult,
                                       ALU.add).then_inc(sm["n_u"], 1)
                wait(dve, "n_u", n + 1)
                v.bn_stats(stat4[:, m, :], u4[:, m, :]).then_inc(sm["n_stat"], 1)

            def out_moments(j):
                wait(dve, "n_stat", TB * (j + 1))
                aggregate4("n_", j)

            def third_norm(j):
                normalise4("n_", lambda m: u4[:, m, :], lambda m: n4[:, m, :], j, "n_nrm")

            def x1_moments(j):
                wait(dve, "n_x1", j + 1)
                moments4("m_", lambda m: y[:, j * TB + m, :], j)

            def h_norm(j):
                normalise4("m_", lambda m: y[:, j * TB + m, :], lambda m: h4[:, m, :], j, "m_h")

            def h_lo(j):
                wait(dve, "m_hhi", j + 1)
                v.tensor_tensor(hs[:, :, 1, :], h4, hs[:, :, 0, :], ALU.subtract).then_inc(sm["m_hlo"], 1)

            recf = recs[:].bitcast(F32)

            def choose(j):
                wait(dve, "r_logit", j + 1)
                link(v.tensor_scalar(lg.rearrange("p m e -> p (m e)"), ps[2][:, :TB * NE], 1.0 / WS, None, ALU.mult))
                for m in range(TB):
                    r = v.max(top[:, m, :], lg[:, m, :])
                link(r)
                for m in range(TB):
                    r = v.max_index(topi[:, m, :], top[:, m, :], lg[:, m, :])
                link(r)
                v.tensor_tensor(dl[:], top[:, :, 1], top[:, :, 0], ALU.subtract).then_inc(sm["r_dl"], 1)
                link(v.tensor_copy(topf[:], topi[:, :, 0:TOP]))
                for c in range(TOP):
                    r = v.tensor_tensor(oh[:, c], iota8[:].unsqueeze(1).broadcast_to([P, TB, NE]),
                                        topf[:, :, c].unsqueeze(2).broadcast_to([P, TB, NE]), ALU.is_equal)
                link(r)
                v.tensor_tensor(cho[:, j * TB:(j + 1) * TB, :], oh[:, 0], oh[:, 1], ALU.add).then_inc(sm["r_cho"], 1)

            def weigh(j):
                b = slice(j * TB, (j + 1) * TB)
                wait(dve, "r_exp", j + 1)
                link(v.tensor_scalar(den[:], ex[:], 1.0, WS, ALU.add, ALU.mult))
                v.reciprocal(recf[:, b, 0, 1], den[:]).then_inc(sm["r_rec"], 1)
                wait(dve, "r_rec", TOP * j + 1)
                v.tensor_tensor(recf[:, b, 1, 1], ex[:], recf[:, b, 0, 1], ALU.mult).then_inc(sm["r_rec"], 1)

            def place(j):
                wait(dve, "r_rank", j + 1)
                link(v.tensor_tensor(slot, ps[3][:, :TB * NE].rearrange("p (m e) -> p m e", m=TB),
                                     ebase[:].unsqueeze(1).broadcast_to([P, TB, NE]), ALU.add))
                for c in range(TOP):
                    link(v.tensor_tensor(prod, slot, oh[:, c], ALU.mult))
                    link(v.tensor_reduce(slotf[:, c, :], prod, X, ALU.add))
                v.tensor_copy(slots[:, :, j * TB:(j + 1) * TB], slotf[:]).then_inc(sm["r_slot"], 1)

            def table():
                wait(dve, "r_count", 1)
                cnt = ps[2][:, CH - NE:]
                link(v.tensor_tensor(used, cnt.unsqueeze(2).broadcast_to([P, NE, NT]),
                                     cuts[:].unsqueeze(1).broadcast_to([P, NE, NT]), ALU.is_gt))
                link(v.tensor_reduce(ntile[:], used, X, ALU.add))
                link(v.tensor_tensor(upto, ntile[:].unsqueeze(1).broadcast_to([P, NE, NE]), tri8[:], ALU.mult))
                link(v.tensor_reduce(icum[:], upto, X, ALU.add))
                n = NE - 1
                link(v.tensor_tensor(past, icum[:, :n].unsqueeze(1).broadcast_to([P, NJ, n]),
                                     jot[:].unsqueeze(2).broadcast_to([P, NJ, n]), ALU.is_le))
                link(v.tensor_scalar(skip[:], ntile[:], -1.0, float(BL), ALU.mult, ALU.add))
                link(v.tensor_tensor(jump, past, skip[:, :n].unsqueeze(1).broadcast_to([P, NJ, n]), ALU.mult))
                link(v.tensor_reduce(tabf[:, 1, :], jump, X, ALU.add))
                link(v.tensor_reduce(tabf[:, 0, :], past, X, ALU.add))
                link(v.tensor_scalar(tab[:, 0, :], tabf[:, 0, :], float(NP), None, ALU.mult))
                v.tensor_tensor(tab[:, 1, :], tabf[:, 1, :], jot[:], ALU.add).then_inc(sm["r_tab"], 1)

            y_lo(0)
            for j in range(NB):
                for f in range(KF):
                    hid_lo(j, f)
                    if f % 2 == 0:
                        split_ff(split_lo, dve, j, (f // 2,))
                    if j:
                        if f == 0:
                            third_norm(j - 1)
                        if f == 4:
                            x1_moments(j - 1)
                        if f == 5:
                            h_norm(j - 1)
                if j:
                    h_lo(j - 1)
                if j + 1 < NB:
                    y_lo(j + 1)
                if j:
                    choose(j - 1)
                out_tile(j, 0)
                out_tile(j, 1)
                if j:
                    weigh(j - 1)
                    place(j - 1)
                out_tile(j, 2)
                out_tile(j, 3)
                out_moments(j)
            j = NB - 1
            third_norm(j)
            x1_moments(j)
            h_norm(j)
            h_lo(j)
            choose(j)
            weigh(j)
            place(j)
            table()

            def gated(n, q):
                dve.wait_ge(sm["e_sil"], n + 1)
                v.scalar_tensor_tensor(act[:, q, :], ps[2 * q + 1][:], 1.0 / WS, sil[:, q, :], ALU.mult,
                                       ALU.mult).then_inc(sm["e_act"], 1)

            def act_lo(n, q):
                dve.wait_ge(sm["e_ahi"], n + 1)
                v.tensor_tensor(actT[:, q, 1, :, :].rearrange("p k t -> p (k t)"), psT[q][:],
                                actT[:, q, 0, :, :].rearrange("p k t -> p (k t)"), ALU.subtract).then_inc(sm["e_alo"], 1)

            def weighted(n, q):
                dve.wait_ge(sm["e_down"], n + 1)
                if not (isinstance(n, int) and n < 2):
                    dve.wait_ge(sm["e_add"], 16 * n - 16)
                v.tensor_scalar(ys[:, q, :], psO[q][:, :D], rec.bitcast(F32)[:, n, 1:2], None,
                                ALU.mult).then_inc(sm["e_y"], 1)

            def e_step(n, q):
                gated(n, q)
                act_lo(n - 1, 1 - q)
                weighted(n - 2, q)

            gated(0, 0)
            gated(1, 1)
            act_lo(0, 0)
            e_step(2, 0)
            e_step(3, 1)
            with dve.Fori(4, NJ - 1, 2) as n:
                e_step(n, 0)
                e_step(n + 1, 1)
            act_lo(NJ - 1, 1)
            weighted(NJ - 2, 0)
            weighted(NJ - 1, 1)


def kernel(**inputs):
    import concourse.bacc as bacc
    from concourse.bass_utils import run_bass_kernel_spmd

    a = {k: np.asarray(v) for k, v in inputs.items()}
    f = "L0_xattn_"
    ctx_ = a["ctx_1024"][0]
    w13 = np.stack([a["L0_ffn_w1"].transpose(0, 2, 1), a["L0_ffn_w3"].transpose(0, 2, 1)], axis=1)
    w13 = w13.reshape(NE, 2, KD, P, NI).transpose(0, 2, 1, 3, 4).reshape(NE, 2 * KD, P, CH)
    w2t = a["L0_ffn_w2"].transpose(0, 2, 1).reshape(NE, KI // 2, 2, P, D).transpose(0, 1, 3, 2, 4)
    arrays = {
        "x_in": a["x"][0],
        "z_in": ctx_,
        "zT_in": ctx_.T,
        "w1_in": a[f + "w1"],
        "w2_in": a[f + "w2"],
        "wgT_in": a["L0_ffn_wg"].T,
        "we_in": np.concatenate([w13, w2t.reshape(NE, KI // 2, P, CH)], axis=1).reshape(NE * NP, P, CH),
        "b1_in": a[f + "b1"].reshape(KF, P).T,
        "rows_in": np.concatenate([a[f + n] for n in ("g1", "beta1", "g2", "beta2", "b2", "g3", "beta3")]),
    }
    arrays = {k: np.ascontiguousarray(v) for k, v in arrays.items()}
    nc = bacc.Bacc("TRN2", target_bir_lowering=False, num_devices=1)
    args = [nc.dram_tensor(k, v.shape, mybir.dt.from_np(v.dtype), kind="ExternalInput").ap()
            for k, v in arrays.items()]
    out = nc.dram_tensor("out", (S + P, D), F32, kind="ExternalOutput").ap()
    xattn_ffn_moe(nc, *args, out)
    r = run_bass_kernel_spmd(nc, [arrays], core_ids=[0])
    return r.results[0]["out"][:S].reshape(1, S, D)
```

```python
import numpy as np
import concourse.bass as bass
from concourse import mybir
from contextlib import ExitStack

F32, F16, U32, I32 = mybir.dt.float32, mybir.dt.float16, mybir.dt.uint32, mybir.dt.int32
ALU = mybir.AluOpType
ACT = mybir.ActivationFunctionType
X = mybir.AxisListType.X

P = 128
S, D = 2048, 256
L = 1601
DFF = 1024
NE, NI = 8, 512
TOP = 2
NT = S // P
KD = D // P
NZ = -(-L // P)
ZR = L - (NZ - 1) * P
KF = DFF // P
KI = NI // P
CH = 4 * P
TB = 4
NB = NT // TB


def full_tiles(blocks):
    return -(-(blocks * TB * TOP * P - NE * (P - 1)) // P)


PHASES = ((NB - 2, 0, full_tiles(NB - 2)),
          (NB - 1, full_tiles(NB - 2), full_tiles(NB - 1)),
          (NB, full_tiles(NB - 1), (TOP * S + NE * (P - 1)) // P))
EPS = 1e-5
WS = 64.0
SM = float(D) ** -0.5
MASKED = -60000.0
NP = KD * 2 + KI * D // CH
NJ = (TOP * S + NE * (P - 1)) // P
BL = NT
LISTS = (NE - 1) * BL + NJ
PW = 832

PARTS = ((0, 0), (0, 1), (1, 0))


def xattn_ffn_moe(nc, x, z, zT, w1, w2, wgT, we, b1, rows, out):
    with ExitStack() as ctx:
        def sb(name, shape, dt=F32):
            return ctx.enter_context(nc.sbuf_tensor(name, shape, dt))

        def sem(name):
            return ctx.enter_context(nc.semaphore(name))

        hrow = nc.dram_tensor("hrow", (S + P, 2 * D), F16, kind="Internal").ap()
        lists = nc.dram_tensor("lists", (LISTS * P, 2), U32, kind="Internal").ap()

        ident = sb("ident", [P, P])
        ident16 = sb("ident16", [P, P], F16)
        mask = sb("mask", [P, P], F16)
        tri = sb("tri", [P, P], F16)
        ones = sb("ones", [P, P], F16)
        expo = sb("expo", [P, TB])
        bridge = sb("bridge", [P, 3])
        iota8 = sb("iota8", [P, NE])
        ebase = sb("ebase", [P, NE])
        cuts = sb("cuts", [P, NT])
        cutf = sb("cutf", [P, NT])
        tri8 = sb("tri8", [P, NE, NE])
        jot = sb("jot", [P, NJ])
        vec = sb("vec", [P, 5, D])
        b1c = sb("b1c", [P, KF])
        w1m = sb("w1m", [P, KD * DFF])
        w2s = sb("w2s", [P, 2, KF, D], F16)
        wgs = sb("wgs", [P, 2, KD, NE], F16)
        w1s = w1m[:].bitcast(F16).rearrange("p (a k f) -> p a k f", a=2, k=KD)
        arena = sb("arena", [P, NE * NP * 2 * CH], F16)
        ew = arena[:].rearrange("p (n a c) -> p n a c", a=2, c=CH)
        NA = NE * NP * 2 * CH
        yv = arena[:, :2 * NT * D].rearrange("p (a t d) -> p a t d", a=2, t=NT)
        z0 = NA - 2 * NZ * D - 2 * KD * L
        zs = arena[:, z0:z0 + 2 * NZ * D].rearrange("p (a t d) -> p a t d", a=2, t=NZ)
        zTs = arena[:, z0 + 2 * NZ * D:].rearrange("p (a k l) -> p a k l", a=2, k=KD)
        FREE0 = -(-2 * NT * D // (2 * CH))
        FREE1 = z0 // (2 * CH)
        y = sb("y", [P, NT, D])
        xin = sb("xin", [P, 2, TB, D])
        tT = sb("tT", [P, 2 * KD * NT * P], F16)
        yT = tT[:].rearrange("p (a k t c) -> p a k t c", a=2, k=KD, t=NT)
        hidT = tT[:].rearrange("p (a f c) -> p a f c", a=2, f=KF)
        prob = sb("prob", [P, 2, NT * P])
        probT = sb("probT", [P, 2, 2, NT, P], F16)
        stage = sb("stage", [P, 2, PW])
        pf = prob[:].rearrange("p a b -> p (a b)")
        hid = pf[:, 0:4 * CH].rearrange("p (q c) -> p q c", q=4)
        u4 = pf[:, 2048:3072].rearrange("p (m d) -> p m d", m=TB)
        h4 = pf[:, 3072:4096].rearrange("p (m d) -> p m d", m=TB)
        ph = probT[:].rearrange("p s a t c -> p (s a t c)")
        ybT = ph[:, 0:2048].rearrange("p (a k c) -> p a k c", a=2, k=KD)
        hs = ph[:, 2048:4096].rearrange("p (m a d) -> p m a d", m=TB, a=2)
        hT = ph[:, 4096:6144].rearrange("p (m a k c) -> p m a k c", m=TB, a=2, k=KD)
        actT = tT[:, 0:2048].rearrange("p (q a k c) -> p q a k c", q=2, a=2, k=KI)
        xg = stage[:, :, CH:CH + D].bitcast(F16)
        xT = tT[:, 3072:4096].rearrange("p (q b c) -> p q b c", q=2, b=2 * KD)
        sil = w1m[:, 0:2 * NI].rearrange("p (q c) -> p q c", q=2)
        act = w1m[:, 2 * NI:4 * NI].rearrange("p (q c) -> p q c", q=2)
        ys = stage[:, :, :D]
        qst = sb("qst", [P, 2, D])
        qT = sb("qT", [P, 2, 2, KD, P], F16)
        zero = qT[:].rearrange("p q a k c -> p (q a k c)")[:, :2 * D]
        u = sb("u", [P, 2, D])
        nrm = sb("nrm", [P, 2, D])
        cmax = sb("cmax", [P, 2, 4])
        nmax = sb("nmax", [P, 2, 1])
        nbias = sb("nbias", [P, 2, 1])
        esum = sb("esum", [P, 2, 4])
        rsum = sb("rsum", [P, 2, 1])
        rinv = sb("rinv", [P, 2, 1])
        stat = sb("stat", [P, 2, 6])
        mv = sb("mv", [P, 2, 2])
        veps = sb("veps", [P, 2, 1])
        rstd = sb("rstd", [P, 2, 1])
        stat4 = sb("stat4", [P, TB, 6])
        mv4 = sb("mv4", [P, TB, 2])
        veps4 = sb("veps4", [P, TB])
        rstd4 = sb("rstd4", [P, TB])
        topf = sb("topf", [P, TB, TOP])
        dl = sb("dl", [P, TB])
        ex = sb("ex", [P, TB])
        den = sb("den", [P, TB])
        cho = sb("cho", [P, NT, NE], F16)
        slotf = sb("slotf", [P, TOP, TB])
        slots = sb("slots", [P, TOP, NT], U32)
        recs = sb("recs", [P, NT, TOP, 2], U32)
        ntile = sb("ntile", [P, NE])
        icum = sb("icum", [P, NE])
        rem = sb("rem", [P, NE])
        taken = sb("taken", [P, NE])
        more = sb("more", [P, NE])
        skip = sb("skip", [P, NE])


        def inside(buf, at, shape, dt=F32):
            n = int(np.prod(shape[1:]))
            v = buf[:].rearrange("p a b -> p (a b)")[:, at:at + n].bitcast(dt)
            names = " ".join("abc"[:len(shape) - 1])
            return v.rearrange(f"p ({names}) -> p {names}", **{k: d for k, d in zip("abc", shape[1:])})

        fill = inside(qst, 0, [P, LISTS, 2], U32)
        lg = inside(u, 0, [P, TB, NE])
        top = inside(u, 32, [P, TB, 8])
        topi = inside(u, 64, [P, TB, 8], U32)
        oh = inside(u, 96, [P, TOP, TB, NE])
        slot = inside(u, 160, [P, TB, NE])
        prod = inside(u, 192, [P, TB, NE])
        jump = inside(u, 224, [P, NJ, NE - 1])
        used = inside(nrm, 0, [P, NE, NT])
        upto = inside(nrm, 128, [P, NE, NE])
        past = inside(nrm, 192, [P, NJ, NE - 1])
        tabf = inside(qst, 0, [P, 2, NJ])
        tab = inside(qst, 2 * NJ, [P, 2, NJ], U32)
        rec = inside(qst, 4 * NJ, [P, NJ, 2], U32)

        ps = [ctx.enter_context(nc.psum_tensor(f"ps{n}", [P, CH], F32)) for n in range(8)]
        psT = ps[4:6]
        psO = ps[6:8]

        names = """vec_in b1_in x_in0 x_in1 x_in2 x_in3 consts fill_made stage_in0 stage_in1 st_hi st_lo
            l0_stat l0_agg l0_var l0_rstd l0_nrm l0_vhi l0_vlo l0_tr l0_hi l0_lo
            s_scores s_cmax s_nmax s_bias s_exp s_tr s_hi s_lo s_pv s_rsum s_rinv s_u s_stat s_agg s_var
            s_rstd s_nrm s_gam s_y
            c_scores c_cmax c_nmax c_bias c_exp c_tr c_hi c_lo c_pv c_rsum c_rinv c_u c_stat c_agg c_var
            c_rstd c_nrm c_gam c_y c_qst c_qtr c_qhi c_qlo
            f_ytr f_yhi f_ylo f_up f_hi f_lo f_down f_xb
            n_yb n_u n_stat n_agg n_var n_rstd n_cen n_x1 x2_in0 x2_in1
            m_stat m_agg m_var m_rstd m_h m_hhi m_hlo h_tr h_cp r_logit r_lg r_rk r_used r_dl r_exp r_cho r_rank r_slot r_rec
            h_out x1_out fill_out rec_out r_count r_tab chain
            rec_in0 rec_in1 rec_in2 rec_in3 e_x0 e_x1 e_xtr e_xcp e_up e_sil e_act e_tr e_ahi e_alo e_down e_y
            e_add""".split()
        sm = {n: sem(n) for n in names}

        def wide(n, a=None):
            return (lambda q: stage[:, q, :n]) if a is None else \
                   (lambda q: stage[:, q, :n].rearrange("p (a n) -> p a n", a=a))

        pieces = []
        for t in range(0, NZ - 1, 2):
            pieces.append((z[t * P:(t + 2) * P, :].rearrange("(a p) d -> p a d", p=P), wide(2 * D, 2),
                           zs[:, 0, t:t + 2, :], zs[:, 1, t:t + 2, :], 1.0))
        pieces.append((z[(NZ - 1) * P:L, :], lambda q: stage[:ZR, q, :D], zs[:ZR, 0, NZ - 1, :],
                       zs[:ZR, 1, NZ - 1, :], 1.0))
        for k in range(KD):
            for a, b in ((0, L // 2), (L // 2, L)):
                pieces.append((zT[k * P:(k + 1) * P, a:b], wide(b - a), zTs[:, 0, k, a:b], zTs[:, 1, k, a:b], 1.0))
        for k in range(KD):
            for a in range(0, DFF, CH):
                pieces.append((w1[k * P:(k + 1) * P, a:a + CH], wide(CH), w1s[:, 0, k, a:a + CH],
                               w1s[:, 1, k, a:a + CH], WS))
        for k in range(0, KF, 2):
            pieces.append((w2[k * P:(k + 2) * P, :].rearrange("(a p) d -> p a d", p=P), wide(2 * D, 2),
                           w2s[:, 0, k:k + 2, :], w2s[:, 1, k:k + 2, :], WS))
        pieces.append((wgT.rearrange("(k p) e -> p k e", p=P), wide(KD * NE, KD), wgs[:, 0], wgs[:, 1], WS))

        def expert_piece(n):
            return (we[n, :, :] if isinstance(n, int) else we[bass.ds(n, 1), :, :].rearrange("a p c -> p (a c)"),
                    wide(CH), ew[:, n, 0, :], ew[:, n, 1, :], WS)

        N_SELF = 2 * NT - 4
        first = 2 * NP
        for n in range(first, first + N_SELF - len(pieces)):
            pieces.append(expert_piece(n))
        second = n + 1
        assert first >= FREE0
        LAST = 2 * NP - 1
        assert second - 1 + NT - 1 < FREE1
        rest = list(range(second + NT - 1, NE * NP))

        def wait(eng, name, n):
            eng.wait_ge(sm[name], n)

        def split_load(sp, piece, g, q):
            if not (isinstance(g, int) and g < 2):
                sp.wait_ge(sm["st_lo"], g - 1)
            sp.dma_start(piece[1](q), piece[0]).then_inc(sm[f"stage_in{q}"], 16)

        def split_hi(act_, piece, g, q):
            act_.wait_ge(sm[f"stage_in{q}"], 8 * (g - q) + 16)
            nc.scalar.activation(piece[2], piece[1](q), ACT.Copy, scale=piece[4]).then_inc(sm["st_hi"], 1)

        def split_lo(dve, piece, g, q):
            dve.wait_ge(sm["st_hi"], g + 1)
            nc.vector.scalar_tensor_tensor(piece[3], piece[1](q), piece[4], piece[2], ALU.mult,
                                           ALU.subtract).then_inc(sm["st_lo"], 1)

        def split_cross(fn, eng, s):
            if isinstance(s, int) and s > LAST:
                g = N_SELF + LAST + s
                fn(eng, expert_piece(s + (second - 1)), g, g % 2)
                return
            if isinstance(s, int) and s == 0:
                fn(eng, expert_piece(0), N_SELF, 0)
                return
            fn(eng, expert_piece(s), 2 * s + (N_SELF - 1), 1)
            fn(eng, expert_piece(s + (second - 1)), 2 * s + N_SELF, 0)

        G_FF = N_SELF + LAST + NT
        per = -(-len(rest) // NB)

        def split_ff(fn, eng, j, some=None):
            for m, n in enumerate(rest[j * per:(j + 1) * per]):
                g = G_FF + j * per + m
                if some is None or m in some:
                    fn(eng, expert_piece(n), g, g % 2)

        def bridge_dve():
            nc.vector.memset(bridge[:, 0:1], 0.0)

        def bridge_pool(col):
            nc.gpsimd.tensor_tensor(bridge[:, col:col + 1], expo[:, 0:1], expo[:, 0:1], ALU.mult)

        def chunk_of(i):
            return -(-(i + 1) // 4)

        EARLY = 4
        S_CH = [0]
        for i in range(NT):
            S_CH.append(S_CH[-1] + chunk_of(i))
        C_CH = -(-L // CH)
        CW = [CH] * (C_CH - 1) + [L - CH * (C_CH - 1)]
        L0_STATS = {0: 2, 2: 3}
        L0_NORM = {1: 2, 3: 3}
        L0_TRANS = {0: 1, 2: 2, 4: 3}
        L0_VLO = {1: 1, 3: 2, 5: 3}
        SPLITS = [0, 0] + [2] * (NT - 2)
        RANKS2_AT, H_AT, LOGITS_AT, RANKS_AT = 2, 6, 8, 10
        E_LOOP = RANKS_AT + 2
        LOOP = (2, NT - 4)

        def psY(j):
            return psT if j else ps[2:4]

        block = ctx.enter_context(nc.Block())

        def store_x1(sp, j):
            wait(sp, "n_x1", j + 1)
            sp.dma_start(out[j * TB * P:(j + 1) * TB * P, :].rearrange("(m p) d -> p m d", p=P),
                         y[:, j * TB:(j + 1) * TB, :]).then_inc(sm["x1_out"], 16)

        def store_h(sp, j):
            wait(sp, "m_hlo", j + 1)
            sp.dma_start(hrow[j * TB * P:(j + 1) * TB * P, :].rearrange("(m p) c -> p m c", p=P),
                         hs.rearrange("p m a d -> p m (a d)")).then_inc(sm["h_out"], 16)

        @block.sync
        def _(sp):
            def load_x(b, name):
                sp.dma_start(xin[:, b % 2], x[b * TB * P:(b + 1) * TB * P, :].rearrange("(m p) d -> p m d", p=P)
                             ).then_inc(sm[name + str(b % 2)], 16)

            for b in range(NB):
                sp.dma_start(y[:, b * TB:(b + 1) * TB, :],
                             x[b * TB * P:(b + 1) * TB * P, :].rearrange("(m p) d -> p m d", p=P)
                             ).then_inc(sm[f"x_in{b}"], 16)
            split_load(sp, pieces[0], 0, 0)
            split_load(sp, pieces[1], 1, 1)
            sp.dma_start(vec[:].rearrange("p a d -> p (a d)"), rows[:5 * D].partition_broadcast(P)).then_inc(sm["vec_in"], 16)
            sp.dma_start(b1c[:], b1).then_inc(sm["b1_in"], 16)
            wait(sp, "fill_made", 3)
            sp.dma_start(lists.rearrange("(p r) c -> p (r c)", p=P), fill.rearrange("p r c -> p (r c)")
                         ).then_inc(sm["fill_out"], 16)
            sp.dma_start(hrow[S:S + P, :], zero).then_inc(sm["fill_out"], 16)
            sp.dma_start(out[S:S + P, :], zero.bitcast(F32)).then_inc(sm["fill_out"], 16)
            for g in range(2, N_SELF):
                split_load(sp, pieces[g], g, g % 2)
            split_cross(split_load, sp, 0)
            split_cross(split_load, sp, 1)
            wait(sp, "s_y", NT)
            sp.dma_start(vec[:, 0:2, :].rearrange("p a d -> p (a d)"), rows[5 * D:].partition_broadcast(P)
                         ).then_inc(sm["vec_in"], 16)
            for b in range(2):
                load_x(b, "x2_in")
            with sp.Fori(LOOP[0], LOOP[1] - 1, 2) as i:
                split_cross(split_load, sp, i)
                split_cross(split_load, sp, i + 1)
            for s in range(LOOP[1], NT):
                split_cross(split_load, sp, s)
            def load_rec(n, q):
                at = sp.value_load(tab[0:1, 1, bass.ds(n, 1)], min_val=0, max_val=LISTS - 1)
                sp.dma_start(rec[:, n, :], lists[bass.ds(at * P, P), :]).then_inc(sm[f"rec_in{q}"], 16)

            def load_recs(phase):
                blocks, n0, n1 = PHASES[phase]
                wait(sp, "r_tab", phase + 1)
                wait(sp, "rec_out", 16 * TOP * TB * blocks)
                looped = (n1 - n0) // 4 * 4 if n1 - n0 > 8 else 0
                if looped:
                    with sp.Fori(n0, n0 + looped - 3, 4) as n:
                        for q in range(4):
                            slot_ = (n0 + q) % 4
                            sp.wait_ge(sm[f"rec_in{slot_}"], 4 * n + 4 * (q - slot_))
                            load_rec(n + q, slot_)
                for n in range(n0 + looped, n1):
                    if n >= 4:
                        wait(sp, f"rec_in{n % 4}", 16 * (n // 4))
                    load_rec(n, n % 4)

            for j in range(NB):
                if j:
                    store_x1(sp, j - 1)
                    if j + 1 < NB:
                        load_x(j + 1, "x2_in")
                split_ff(split_load, sp, j)
                if j:
                    store_h(sp, j - 1)
            load_recs(0)
            store_x1(sp, NB - 1)
            store_h(sp, NB - 1)
            load_recs(1)
            load_recs(2)
            wait(sp, "e_add", 16 * NJ)

        @block.gpsimd
        def _(pool):
            g = nc.gpsimd
            inc = lambda r: r.then_inc(sm["consts"], 1)
            inc(g.memset(ident[:], 0.0))
            inc(g.memset(ident16[:], 0.0))
            inc(g.memset(mask[:], 0.0))
            inc(g.memset(expo[:], -0.5))
            inc(g.memset(ones[:], 1.0))
            inc(g.memset(tri[:], 1.0))
            wait(pool, "consts", 6)
            for t in (ident, ident16):
                inc(g.affine_select(out=t[:], in_=t[:], compare_op=ALU.not_equal, fill=1.0, base=0,
                                    pattern=[[-1, P]], channel_multiplier=1))
            inc(g.affine_select(out=mask[:], in_=mask[:], compare_op=ALU.is_ge, fill=MASKED, base=0,
                                pattern=[[-1, P]], channel_multiplier=1))

            def l0_rstd(b):
                wait(pool, "l0_var", b + 1)
                g.tensor_tensor(rstd4[:], veps4[:], expo[:], ALU.pow).then_inc(sm["l0_rstd"], 1)

            def l0_vlo(b):
                wait(pool, "l0_vhi", b + 1)
                g.tensor_tensor(yv[:, 1, b * TB:(b + 1) * TB, :], y[:, b * TB:(b + 1) * TB, :],
                                yv[:, 0, b * TB:(b + 1) * TB, :], ALU.subtract).then_inc(sm["l0_vlo"], 1)

            l0_rstd(0)
            l0_rstd(1)
            l0_vlo(0)
            iota = lambda o, pat, base=0, mult=0: inc(g.iota(o, pattern=pat, base=base, channel_multiplier=mult,
                                                             allow_small_or_imprecise_dtypes=True))
            inc(g.affine_select(out=tri[:], in_=tri[:], compare_op=ALU.is_gt, fill=0.0, base=0,
                                pattern=[[1, P]], channel_multiplier=-1))
            iota(iota8[:], [[1, NE]])
            iota(ebase[:], [[BL * P, NE]])
            iota(cuts[:], [[P, NT]])
            iota(cutf[:], [[P, NT]], P - 1)
            iota(jot[:], [[1, NJ]])
            iota(recs[:].rearrange("p t c w -> p t (c w)"), [[P, NT], [0, 2 * TOP]], 0, 1)
            iota(fill, [[1, LISTS], [0, 2]], 0, LISTS)
            inc(g.memset(tri8[:], 1.0))
            wait(pool, "consts", 18)
            inc(g.affine_select(out=tri8[:], in_=tri8[:], compare_op=ALU.is_ge, fill=0.0, base=0,
                                pattern=[[1, NE], [-1, NE]], channel_multiplier=0))

            def ln_rstd(pre, i, q):
                pool.wait_ge(sm[pre + "var"], i + 1)
                g.tensor_tensor(rstd[:, q, :], veps[:, q, :], expo[:, 0:1], ALU.pow).then_inc(sm[pre + "rstd"], 1)

            def ln_affine(pre, i, q, row):
                pool.wait_ge(sm[pre + "nrm"], i + 1)
                g.tensor_tensor(nrm[:, q, :], nrm[:, q, :], vec[:, row, :], ALU.mult).then_inc(sm[pre + "gam"], 1)
                pool.wait_ge(sm[pre + "gam"], i + 1)
                if not isinstance(i, int):
                    bridge_pool(1)
                g.tensor_tensor(y[:, i, :], nrm[:, q, :], vec[:, row + 1, :], ALU.add).then_inc(sm[pre + "y"], 1)

            def q_stage(t, q):
                if not (isinstance(t, int) and t < 2):
                    pool.wait_ge(sm["c_qtr"], t - 1)
                    if not isinstance(t, int):
                        bridge_pool(2)
                g.tensor_copy(qst[:, q, :], y[:, t, :]).then_inc(sm["c_qst"], 1)

            wait(pool, "vec_in", 16)
            for i in range(1, NT):
                if i - 1 in L0_STATS:
                    l0_rstd(L0_STATS[i - 1])
                ln_rstd("s_", i - 1, (i - 1) % 2)
                ln_affine("s_", i - 1, (i - 1) % 2, 0)
                if i in L0_VLO:
                    l0_vlo(L0_VLO[i])
                if i == NT - 3:
                    wait(pool, "fill_out", 48)
                    wait(pool, "s_y", 2)
                    q_stage(0, 0)
                    q_stage(1, 1)
            q_stage(2, 0)
            ln_rstd("s_", NT - 1, (NT - 1) % 2)
            ln_affine("s_", NT - 1, (NT - 1) % 2, 0)

            def c_step(i, q):
                if not isinstance(i, int) or i + 3 < NT:
                    q_stage(i + 3, 1 - q)
                ln_rstd("c_", i, q)
                ln_affine("c_", i, q, 2)

            for i in range(LOOP[0]):
                c_step(i, i % 2)
            with pool.Fori(LOOP[0], LOOP[1] - 1, 2) as i:
                c_step(i, 0)
                c_step(i + 1, 1)
            for i in range(LOOP[1], NT):
                c_step(i, i % 2)
            wait(pool, "c_y", NT)

            def bc(row, n=TB):
                return vec[:, row, :].unsqueeze(1).broadcast_to([P, n, D])

            def blk(j):
                return y[:, j * TB:(j + 1) * TB, :]

            def x_beta(j):
                wait(pool, f"x2_in{j % 2}", 16 * (j // 2 + 1))
                g.tensor_tensor(xin[:, j % 2], xin[:, j % 2], bc(1), ALU.add).then_inc(sm["f_xb"], 1)

            def y_b2(j):
                wait(pool, "f_ytr", j + 1)
                g.tensor_tensor(blk(j), blk(j), bc(4), ALU.add).then_inc(sm["n_yb"], 1)

            def rstd_of(pre, j):
                wait(pool, pre + "var", j + 1)
                g.tensor_tensor(rstd4[:], veps4[:], expo[:], ALU.pow).then_inc(sm[pre + "rstd"], 1)

            def scatter(j, ms):
                wait(pool, "r_slot", j + 1)
                wait(pool, "r_rec", TOP * (j + 1))
                for m in ms:
                    for c in range(TOP):
                        t = j * TB + m
                        g.indirect_dma_start(lists, bass.IndirectOffsetOnAxis(slots[:, c, t:t + 1], 0),
                                             recs[:, t, c, :], None).then_inc(sm["rec_out"], 16)

            wait(pool, "fill_out", 48)
            wait(pool, "vec_in", 32)
            y_b2(0)
            x_beta(0)
            for j in range(NB):
                if j > 1:
                    scatter(j - 2, (0, 1))
                if j:
                    rstd_of("m_", j - 1)
                if j > 1:
                    scatter(j - 2, (2, 3))
                if j + 1 < NB:
                    y_b2(j + 1)
                    x_beta(j + 1)
                    rstd_of("n_", j)

            def phase_of(n):
                return [p for p, (_, n0, n1) in enumerate(PHASES) if n0 <= n < n1][0]

            def rows_of(p):
                return PHASES[p][0] * TB * P if p < 2 else S + P

            def gather(n):
                if n >= 2:
                    wait(pool, "e_xtr", n - 1)
                p = phase_of(n)
                wait(pool, "h_out", 16 * PHASES[p][0])
                wait(pool, f"rec_in{n % 4}", 16 * (n // 4 + 1))
                g.indirect_dma_start(xg[:, n % 2, :], None, hrow[:rows_of(p), :],
                                     bass.IndirectOffsetOnAxis(rec[:, n, 0:1], 0)).then_inc(sm[f"e_x{n % 2}"], 16)

            def add(n):
                p = phase_of(n)
                wait(pool, "x1_out", 16 * PHASES[p][0])
                wait(pool, "e_y", n + 1)
                if n:
                    wait(pool, "e_add", 16 * n)
                g.indirect_dma_start(out[:rows_of(p), :], bass.IndirectOffsetOnAxis(rec[:, n, 0:1], 0),
                                     ys[:, n % 2, :], None, compute_op=ALU.add).then_inc(sm["e_add"], 16)

            def recs_loaded(p):
                for q in range(4):
                    wait(pool, f"rec_in{q}", 16 * ((PHASES[p][2] - q + 3) // 4))

            gather(0)
            gather(1)
            rstd_of("n_", NB - 1)
            gather(2)
            rstd_of("m_", NB - 1)
            for n in range(NJ):
                if n + 3 < NJ:
                    gather(n + 3)
                if n:
                    add(n - 1)
                for j, at in ((NB - 2, RANKS2_AT), (NB - 1, RANKS_AT)):
                    if n == at - 1:
                        recs_loaded(j - (NB - 2))
                    if at - 1 <= n < at - 1 + TB:
                        scatter(j, (n - (at - 1),))
            add(NJ - 1)

        @block.scalar
        def _(act_):
            a = nc.scalar

            def copy(o, i):
                return a.activation(o, i, ACT.Copy)

            def l0_his(b):
                for k in range(KD):
                    wait(act_, "l0_tr", KD * b + k + 1)
                    copy(yT[:, 0, k, b * TB:(b + 1) * TB, :],
                         ps[2 + k][:].rearrange("p (m t) -> p m t", m=TB)).then_inc(sm["l0_hi"], 1)
                copy(yv[:, 0, b * TB:(b + 1) * TB, :], y[:, b * TB:(b + 1) * TB, :]).then_inc(sm["l0_vhi"], 1)

            def exps(pre, q, count, c, w):
                act_.wait_ge(sm[pre + "bias"], count)
                a.activation(prob[:, q, c * CH:c * CH + w], ps[c][:, :w], ACT.Exp, bias=nbias[:, q, :], scale=SM,
                             accum_out=esum[:, q, c:c + 1]).then_inc(sm[pre + "exp"], 1)

            def q_hi(t, q, k):
                act_.wait_ge(sm["c_qtr"], t + 1)
                copy(qT[:, q, 0, :, :], psT[k][:, P:P + D].rearrange("p (k t) -> p k t", k=KD)).then_inc(sm["c_qhi"], 1)

            def c_exps(t, q, c):
                exps("c_", q, t + 1, c, CW[c])

            grp = [0]

            def s_his(i, g):
                n = min(4, i + 1 - 4 * g)
                grp[0] += 1
                wait(act_, "s_tr", grp[0])
                copy(probT[:, i % 2, 0, 4 * g:4 * g + n, :],
                     psT[(grp[0] - 1) % 2][:, :n * P].rearrange("p (k t) -> p k t", k=n)).then_inc(sm["s_hi"], 1)

            def s_exps(i, c):
                exps("s_", i % 2, i + 1, c, min(CH, (i + 1) * P - c * CH))

            l0_his(0)
            s_exps(0, 0)
            for i in range(NT):
                ng = chunk_of(i)
                nch = chunk_of(i + 1) if i + 1 < NT else 0
                for g in range(min(3, ng)):
                    s_his(i, g)
                for n in range(sum(SPLITS[:i]), sum(SPLITS[:i + 1])):
                    split_hi(act_, pieces[n], n, n % 2)
                for c in range(nch):
                    s_exps(i + 1, c)
                    if c == 1 and ng > 3:
                        s_his(i, 3)
                if i == NT - 1:
                    for c in range(C_CH):
                        c_exps(0, 0, c)
                        if c == 1:
                            s_his(i, 3)
                if i in L0_TRANS:
                    l0_his(L0_TRANS[i])
                if i == NT - 2:
                    wait(act_, "fill_out", 48)
                    q_hi(0, 0, 0)
                    q_hi(1, 1, 1)

            def c_his(i, q, g, nxt2=False):
                act_.wait_ge(sm["c_tr"], 4 * i + g + 1)
                if nxt2:
                    act_.wait_ge(sm["c_qtr"], i + 3)
                n = 4 if g < 3 else 1
                r = P if g < 3 else ZR
                copy(probT[:r, q, 0, 4 * g:4 * g + n, :],
                     psT[g % 2][:r, :n * P].rearrange("p (k t) -> p k t", k=n)).then_inc(sm["c_hi"], 1)

            def c_step(i, q, nxt=True, nxt2=True):
                c_his(i, q, 0)
                c_his(i, q, 1)
                c_his(i, q, 2)
                for c in range(C_CH):
                    if c == 2:
                        c_his(i, q, 3, nxt2)
                        if nxt2:
                            q_hi(i + 2, q, 1)
                    if nxt:
                        c_exps(i + 1, 1 - q, c)
                split_cross(split_hi, act_, i)

            for i in range(LOOP[0]):
                c_step(i, i % 2)
            with act_.Fori(LOOP[0], LOOP[1] - 1, 2) as i:
                c_step(i, 0)
                c_step(i + 1, 1)
            for i in range(LOOP[1], NT - 1):
                c_step(i, i % 2, i + 1 < NT, i + 2 < NT)

            def y_hi(j):
                wait(act_, "f_ytr", j + 1)
                for k in range(KD):
                    copy(ybT[:, 0, k, :], psY(j)[k][:]).then_inc(sm["f_yhi"], 1)

            def relu(j, f):
                n = j * KF + f
                wait(act_, "f_up", n + 1)
                a.activation(hidT[:, 0, f, :], ps[f % 2][:], ACT.Relu, bias=b1c[:, f:f + 1], scale=1.0 / WS)
                if n >= 4:
                    wait(act_, "f_lo", n - 3)
                a.activation(hid[:, f % 4, :], ps[f % 2][:], ACT.Relu, bias=b1c[:, f:f + 1],
                             scale=1.0 / WS).then_inc(sm["f_hi"], 1)

            def h_hi(j):
                wait(act_, "m_h", TB * (j + 1))
                if j:
                    wait(act_, "h_out", 16 * j)
                copy(hs[:, :, 0, :], h4).then_inc(sm["m_hhi"], 1)

            def h_copy(j):
                wait(act_, "h_tr", j + 1)
                for n in range(2):
                    copy(hT[:, 2 * n:2 * n + 2].rearrange("p m a k c -> p (m a k c)"),
                         ps[2 + n][:].bitcast(F16)).then_inc(sm["h_cp"], 1)

            def gates(j):
                wait(act_, "r_dl", j + 1)
                a.activation(ex[:], dl[:], ACT.Exp).then_inc(sm["r_exp"], 1)

            wait(act_, "b1_in", 16)
            i = NT - 1
            c_his(i, i % 2, 0)
            c_his(i, i % 2, 1)
            y_hi(0)
            c_his(i, i % 2, 2)
            c_his(i, i % 2, 3)
            split_cross(split_hi, act_, i)
            for f in range(EARLY):
                relu(0, f)
            for j in range(NB):
                for f in range(0 if j else EARLY, KF):
                    relu(j, f)
                    if j > 1 and f == 1:
                        gates(j - 2)
                if j + 1 < NB:
                    y_hi(j + 1)
                split_ff(split_hi, act_, j, (0, 1))
                if j:
                    h_hi(j - 1)
                split_ff(split_hi, act_, j, (2, 3))
                if j:
                    h_copy(j - 1)
            def x_copy(n, q):
                act_.wait_ge(sm["e_xtr"], n + 1)
                copy(xT[:, q, :, :].rearrange("p b c -> p (b c)"), psO[q][:, D:].bitcast(F16)).then_inc(sm["e_xcp"], 1)

            def silu(n, q):
                act_.wait_ge(sm["e_up"], n + 1)
                a.activation(sil[:, q, :], ps[2 * q][:], ACT.Silu, scale=1.0 / WS).then_inc(sm["e_sil"], 1)

            def act_hi(n, q):
                act_.wait_ge(sm["e_tr"], n + 1)
                copy(actT[:, q, 0, :, :].rearrange("p k t -> p (k t)"), psT[q][:]).then_inc(sm["e_ahi"], 1)

            def e_step(n, q, nxt=True):
                silu(n, q)
                act_hi(n - 1, 1 - q)
                if nxt:
                    x_copy(n + 1, 1 - q)

            x_copy(0, 0)
            gates(NB - 2)
            silu(0, 0)
            x_copy(1, 1)
            for n in range(1, E_LOOP):
                silu(n, n % 2)
                if n == H_AT:
                    h_copy(NB - 1)
                act_hi(n - 1, 1 - n % 2)
                x_copy(n + 1, 1 - n % 2)
                if n == H_AT - 1:
                    h_hi(NB - 1)
                if n == LOGITS_AT:
                    gates(NB - 1)
            with act_.Fori(E_LOOP, NJ - 2, 2) as n:
                e_step(n, 0)
                e_step(n + 1, 1)
            e_step(NJ - 1, 0, False)
            act_hi(NJ - 1, 0)

        @block.tensor
        def _(pe):
            t = nc.tensor

            def mm3(o, lhs, rhs, first, last):
                for n, (a, b) in enumerate(PARTS):
                    r = t.matmul(o, lhs(a), rhs(b), start=first and n == 0, stop=last and n == 2)
                return r

            def l0_trans(b):
                if b:
                    wait(pe, "l0_lo", KD * b)
                for m in range(TB):
                    wait(pe, "l0_nrm", TB * b + m + 1)
                    for k in range(KD):
                        r = t.transpose(ps[2 + k][:, m * P:(m + 1) * P], y[:, b * TB + m, k * P:(k + 1) * P], ident[:])
                        if m == TB - 1:
                            r.then_inc(sm["l0_tr"], 1)

            wait(pe, "consts", 9)
            l0_trans(0)

            def q_trans(i, q, k):
                pe.wait_ge(sm["c_qst"], i + 1)
                for m in range(KD):
                    r = t.transpose(psT[k][:, (m + 1) * P:(m + 2) * P], qst[:, q, m * P:(m + 1) * P], ident[:])
                r.then_inc(sm["c_qtr"], 1)

            def c_scores(i, q, cs, first=False):
                if 0 in cs:
                    pe.wait_ge(sm["c_qlo"], i + 1)
                for c in cs:
                    if not first:
                        pe.wait_ge(sm["c_exp"], 4 * i + (c - 3))
                    w = CW[c]
                    for k in range(KD):
                        r = mm3(ps[c][:, :w], lambda a: qT[:, q, a, k, :],
                                lambda b: zTs[:, b, k, c * CH:c * CH + w], k == 0, k == KD - 1)
                    r.then_inc(sm["c_scores"], 1)

            grp = [0]

            def s_scores(i, cs):
                n = chunk_of(i)
                wait(pe, "l0_lo", KD * (NB if n > 2 else i // TB + 1))
                for c in cs:
                    w = min(CH, (i + 1) * P - c * CH)
                    prev = [j for j in range(i) if chunk_of(j) > c]
                    if prev:
                        wait(pe, "s_exp", S_CH[prev[-1]] + c + 1)
                    o = ps[c][:, :w]
                    diag = c == n - 1
                    for k in range(KD):
                        r = mm3(o, lambda a: yT[:, a, k, i, :],
                                lambda b: yT[:, b, k, 4 * c:4 * c + w // P, :],
                                k == 0, k == KD - 1 and not diag)
                    if diag:
                        r = t.matmul(ps[c][:, w - P:w], ident16[:], mask[:], start=False, stop=True)
                    r.then_inc(sm["s_scores"], 1)

            def s_trans(i, g):
                grp[0] += 1
                k = grp[0] - 1
                if k >= 2:
                    wait(pe, "s_lo", k - 1)
                if i == NT - 1 and g == 0:
                    wait(pe, "c_qlo", 2)
                wait(pe, "s_exp", S_CH[i] + g + 1)
                n = min(4, i + 1 - 4 * g)
                for m in range(n):
                    r = t.transpose(psT[k % 2][:, m * P:(m + 1) * P],
                                    prob[:, i % 2, (4 * g + m) * P:(4 * g + m + 1) * P], ident[:])
                r.then_inc(sm["s_tr"], 1)

            def s_pv(i, g):
                wait(pe, "s_lo", S_CH[i] + g + 1)
                if g == 0:
                    wait(pe, "l0_vlo", i // TB + 1)
                    if i >= 2:
                        wait(pe, "s_u", i - 1)
                for m in range(4 * g, min(4 * g + 4, i + 1)):
                    r = mm3(psO[i % 2][:, :D], lambda a: probT[:, i % 2, a, m, :], lambda b: yv[:, b, m, :],
                            m == 0, m == i)
                if 4 * g + 4 >= i + 1:
                    r.then_inc(sm["s_pv"], 1)

            s_scores(0, (0,))
            for i in range(NT):
                ng = chunk_of(i)
                nch = chunk_of(i + 1) if i + 1 < NT else 0
                for g in range(min(2, ng)):
                    s_trans(i, g)
                if i == NT - 1:
                    wait(pe, "st_lo", 11)
                    c_scores(0, 0, (0, 1), True)
                if nch:
                    s_scores(i + 1, range(min(2, nch)))
                if ng > 2:
                    s_trans(i, 2)
                if nch > 2:
                    s_scores(i + 1, range(2, nch))
                if i == NT - 1:
                    c_scores(0, 0, (2, 3), True)
                for g in range(ng):
                    s_pv(i, g)
                    if g == 0 and ng > 3:
                        s_trans(i, 3)
                if i in L0_TRANS:
                    l0_trans(L0_TRANS[i])
                if i == NT - 2:
                    wait(pe, "s_lo", grp[0])
                    q_trans(0, 0, 0)
                    q_trans(1, 1, 1)

            def c_trans(i, q, g):
                if g >= 2 or not (isinstance(i, int) and i == 0):
                    pe.wait_ge(sm["c_lo"], 4 * i + g - 1)
                else:
                    pe.wait_ge(sm["s_lo"], S_CH[NT])
                if g == 1 and not (isinstance(i, int) and i == 0):
                    pe.wait_ge(sm["c_qlo"], min(i + 2, NT) if isinstance(i, int) else i + 2)
                pe.wait_ge(sm["c_exp"], 4 * i + g + 1)
                for m in range(4 * g, min(4 * g + 4, NZ)):
                    r_ = P if m < NZ - 1 else ZR
                    r = t.transpose(psT[g % 2][:r_, (m % 4) * P:(m % 4 + 1) * P],
                                    prob[:, q, m * P:m * P + r_], ident[:])
                r.then_inc(sm["c_tr"], 1)

            def c_pv(i, q, g):
                pe.wait_ge(sm["c_lo"], 4 * i + g + 1)
                if g == 0:
                    if isinstance(i, int) and i < 2:
                        pe.wait_ge(sm["s_u"], NT - 1 + i)
                    else:
                        pe.wait_ge(sm["c_u"], i - 1)
                for m in range(4 * g, min(4 * g + 4, NZ)):
                    r_ = P if m < NZ - 1 else ZR
                    r = mm3(psO[q][:, :D], lambda a: probT[:r_, q, a, m, :], lambda b: zs[:r_, b, m, :],
                            m == 0, m == NZ - 1)
                if g == 3:
                    r.then_inc(sm["c_pv"], 1)

            def c_step(i, q, nxt=True, nxt2=True):
                c_trans(i, q, 0)
                c_trans(i, q, 1)
                if nxt:
                    c_scores(i + 1, 1 - q, (0, 1))
                c_trans(i, q, 2)
                if nxt:
                    c_scores(i + 1, 1 - q, (2, 3))
                c_pv(i, q, 0)
                c_trans(i, q, 3)
                if nxt2:
                    q_trans(i + 2, q, 1)
                c_pv(i, q, 1)
                c_pv(i, q, 2)
                c_pv(i, q, 3)

            for i in range(LOOP[0]):
                c_step(i, i % 2)
            with pe.Fori(LOOP[0], LOOP[1] - 1, 2) as i:
                c_step(i, 0)
                c_step(i + 1, 1)
            for i in range(LOOP[1], NT - 1):
                c_step(i, i % 2, i + 1 < NT, i + 2 < NT)

            def y_trans(j):
                wait(pe, "c_y", TB * (j + 1))
                if j:
                    wait(pe, "c_lo", 4 * NT)
                    wait(pe, "f_ylo", KD * j)
                else:
                    wait(pe, "c_exp", 4 * NT)
                for k in range(KD):
                    for m in range(TB):
                        r = t.transpose(psY(j)[k][:, m * P:(m + 1) * P], y[:, j * TB + m, k * P:(k + 1) * P], ident[:])
                r.then_inc(sm["f_ytr"], 1)

            def ups(j, fs):
                wait(pe, "f_ylo", KD * (j + 1))
                for f in fs:
                    if j > 1 and f == 2:
                        ranks(j - 2)
                        if j == NB - 1:
                            counts(0)
                    if KF * j + f >= 2:
                        wait(pe, "f_hi", KF * j + f - 1)
                    for k in range(KD):
                        r = mm3(ps[f % 2][:], lambda a: w1s[:, a, k, f * P:(f + 1) * P], lambda b: ybT[:, b, k, :],
                                k == 0, k == KD - 1)
                    r.then_inc(sm["f_up"], 1)

            def down(j, m):
                n = j * TB + m
                if n >= 2:
                    wait(pe, "n_u", n - 1)
                for f in range(KF):
                    if m == 0:
                        wait(pe, "f_lo", KF * j + f + 1)
                    r = mm3(psO[m % 2][:, :D], lambda a: hidT[:, a, f, m * P:(m + 1) * P], lambda b: w2s[:, b, f, :],
                            f == 0, f == KF - 1)
                r.then_inc(sm["f_down"], 1)

            def h_trans(j):
                wait(pe, "m_hlo", j + 1)
                if j:
                    wait(pe, "r_rk", j)
                if j > NB - 3:
                    wait(pe, "r_used", j - (NB - 3))
                for m in range(TB):
                    for a in range(2):
                        for k in range(KD):
                            c = ((m % 2) * 2 * KD + a * KD + k) * P
                            r = t.transpose(ps[2 + m // 2][:].bitcast(F16)[:, c:c + P],
                                            hs[:, m, a, k * P:(k + 1) * P], ident16[:])
                r.then_inc(sm["h_tr"], 1)

            def logits(j):
                wait(pe, "h_cp", 2 * (j + 1))
                for m in range(TB):
                    for k in range(KD):
                        r = mm3(ps[2][:, m * NE:(m + 1) * NE], lambda a: hT[:, m, a, k, :], lambda b: wgs[:, b, k, :],
                                k == 0, k == KD - 1)
                r.then_inc(sm["r_logit"], 1)

            def ranks(j):
                wait(pe, "consts", 19)
                wait(pe, "r_cho", j + 1)
                for m in range(TB):
                    n = j * TB + m
                    o = ps[3][:, m * NE:(m + 1) * NE]
                    r = t.matmul(o, tri[:], cho[:, n, :], start=True, stop=n == 0)
                    for b in range(n):
                        r = t.matmul(o, ones[:], cho[:, b, :], start=False, stop=b == n - 1)
                r.then_inc(sm["r_rank"], 1)

            def counts(p):
                tiles = PHASES[p][0] * TB
                for n in range(tiles):
                    r = t.matmul(ps[2][:, CH - NE:], ones[:], cho[:, n, :], start=n == 0, stop=n == tiles - 1)
                r.then_inc(sm["r_count"], 1)

            i = NT - 1
            c_trans(i, i % 2, 0)
            c_trans(i, i % 2, 1)
            y_trans(0)
            c_pv(i, i % 2, 0)
            c_trans(i, i % 2, 2)
            c_pv(i, i % 2, 1)
            c_trans(i, i % 2, 3)
            wait(pe, "st_lo", N_SELF)
            ups(0, (0, 1))
            c_pv(i, i % 2, 2)
            c_pv(i, i % 2, 3)
            ups(0, (2, 3))
            for j in range(NB):
                ups(j, range(0 if j else EARLY, KF))
                if not j:
                    wait(pe, "c_u", NT)
                if j + 1 < NB:
                    y_trans(j + 1)
                down(j, 0)
                down(j, 1)
                down(j, 2)
                if j:
                    h_trans(j - 1)
                down(j, 3)
                if j:
                    logits(j - 1)

            def x_trans(n, q):
                pe.wait_ge(sm[f"e_x{q}"], 8 * (n - q) + 16)
                if not (isinstance(n, int) and n < 4):
                    pe.wait_ge(sm["e_y"], n - 3)
                for b in range(2 * KD):
                    r = t.transpose(psO[q][:, D:].bitcast(F16)[:, b * P:(b + 1) * P], xg[:, q, b * P:(b + 1) * P],
                                    ident16[:])
                r.then_inc(sm["e_xtr"], 1)

            def e_ups(n, q):
                at = pe.value_load(tab[0:1, 0, bass.ds(n, 1)], min_val=0, max_val=(NE - 1) * NP)
                pe.wait_ge(sm["e_xcp"], n + 1)
                if not (isinstance(n, int) and n < 2):
                    pe.wait_ge(sm["e_act"], n - 1)
                for h in range(2):
                    for k in range(KD):
                        r = mm3(ps[2 * q + h][:], lambda a: xT[:, q, a * KD + k, :],
                                lambda b: ew[:, at + (k * 2 + h), b, :], k == 0, k == KD - 1)
                r.then_inc(sm["e_up"], 1)

            def e_trans(n, q):
                pe.wait_ge(sm["e_act"], n + 1)
                if not (isinstance(n, int) and n < 2):
                    pe.wait_ge(sm["e_alo"], n - 1)
                for k in range(KI):
                    r = t.transpose(psT[q][:, k * P:(k + 1) * P], act[:, q, k * P:(k + 1) * P], ident[:])
                r.then_inc(sm["e_tr"], 1)

            def e_downs(n, q, nxt=2):
                at = pe.value_load(tab[0:1, 0, bass.ds(n, 1)], min_val=0, max_val=(NE - 1) * NP)
                pe.wait_ge(sm["e_alo"], n + 1)
                if nxt:
                    pe.wait_ge(sm["e_xcp"], n + 1 + nxt)
                for k in range(KI):
                    r = mm3(psO[q][:, :D], lambda a: actT[:, q, a, k, :],
                            lambda b: ew[:, at + (2 * KD + k // 2), b, (k % 2) * D:(k % 2 + 1) * D],
                            k == 0, k == KI - 1)
                r.then_inc(sm["e_down"], 1)

            wait(pe, "r_tab", 1)
            wait(pe, "r_rk", NB - 2)
            wait(pe, "r_used", 1)
            wait(pe, "n_u", NT)
            wait(pe, "st_lo", G_FF + len(rest))
            x_trans(0, 0)
            e_ups(0, 0)
            x_trans(1, 1)
            wait(pe, "r_lg", NB - 1)
            e_ups(1, 1)
            e_trans(0, 0)
            x_trans(2, 0)

            def e_step(n, q, nxt=True, between=None, banks=None):
                if banks:
                    banks()
                e_ups(n, q)
                if between:
                    wait(pe, "e_act", n)
                    between()
                e_trans(n - 1, 1 - q)
                if nxt:
                    x_trans(n + 1, 1 - q)
                e_downs(n - 2, q)

            def routed(j):
                ranks(j)
                counts(j - (NB - 3))

            def routing_read(j):
                wait(pe, "r_rk", j + 1)
                wait(pe, "r_used", j - (NB - 3) + 1)

            work = {RANKS2_AT: lambda: routed(NB - 2), H_AT: lambda: h_trans(NB - 1),
                    LOGITS_AT: lambda: logits(NB - 1), RANKS_AT: lambda: routed(NB - 1)}
            read = {RANKS2_AT: lambda: routing_read(NB - 2), H_AT: lambda: wait(pe, "h_cp", 2 * NB),
                    LOGITS_AT: lambda: wait(pe, "r_lg", NB), RANKS_AT: lambda: routing_read(NB - 1)}
            for n in range(2, E_LOOP):
                e_step(n, n % 2, True, work.get(n), read.get(n - 1))
            with pe.Fori(E_LOOP, NJ - 2, 2) as n:
                e_step(n, 0)
                e_step(n + 1, 1)
            e_step(NJ - 1, 0, False)
            e_trans(NJ - 1, 0)
            e_downs(NJ - 2, 1, 0)
            e_downs(NJ - 1, 0, 0)

        @block.vector
        def _(dve):
            v = nc.vector
            links = [0]

            def link(ins):
                links[0] += 1
                ins.then_inc(sm["chain"], 1)
                dve.wait_ge(sm["chain"], links[0])

            def normalise(pre, src, q, i):
                dve.wait_ge(sm[pre + "rstd"], i + 1)
                v.tensor_scalar(nrm[:, q, :], src, mv[:, q, 0:1], rstd[:, q, :], ALU.subtract,
                                ALU.mult).then_inc(sm[pre + "nrm"], 1)

            def aggregate4(pre, b):
                for m in range(TB):
                    v.bn_aggr(mv4[:, m, :], stat4[:, m, :]).then_inc(sm[pre + "agg"], 1)
                wait(dve, pre + "agg", TB * (b + 1))
                v.tensor_scalar(veps4[:], mv4[:, :, 1], EPS, None, ALU.add).then_inc(sm[pre + "var"], 1)

            def normalise4(pre, src, dst, b, done):
                wait(dve, pre + "rstd", b + 1)
                for m in range(TB):
                    v.tensor_scalar(dst(m), src(m), mv4[:, m, 0:1], rstd4[:, m:m + 1], ALU.subtract,
                                    ALU.mult).then_inc(sm[done], 1)

            def l0_stats(b, parts=(0, 1)):
                if 0 in parts:
                    wait(dve, f"x_in{b}", 16)
                    for m in range(TB):
                        v.bn_stats(stat4[:, m, :], y[:, b * TB + m, :]).then_inc(sm["l0_stat"], 1)
                if 1 in parts:
                    wait(dve, "l0_stat", TB * (b + 1))
                    if b:
                        wait(dve, "l0_nrm", TB * b)
                    aggregate4("l0_", b)

            def l0_norm(b):
                tile = lambda m: y[:, b * TB + m, :]
                normalise4("l0_", tile, tile, b, "l0_nrm")

            def l0_los(b):
                for k in range(KD):
                    wait(dve, "l0_hi", KD * b + k + 1)
                    v.tensor_tensor(yT[:, 1, k, b * TB:(b + 1) * TB, :],
                                    ps[2 + k][:].rearrange("p (m t) -> p m t", m=TB),
                                    yT[:, 0, k, b * TB:(b + 1) * TB, :], ALU.subtract).then_inc(sm["l0_lo"], 1)

            l0_stats(0)
            l0_stats(1, (0,))
            l0_norm(0)
            l0_stats(1, (1,))
            l0_los(0)

            def maxes(pre, q, c, w, scores):
                dve.wait_ge(sm[pre + "scores"], scores)
                v.tensor_reduce(cmax[:, q, c:c + 1], ps[c][:, :w], X, ALU.max).then_inc(sm[pre + "cmax"], 1)

            def bias(pre, q, n, i, count):
                dve.wait_ge(sm[pre + "cmax"], count)
                v.tensor_reduce(nmax[:, q, :], cmax[:, q, :n], X, ALU.max, negate=True).then_inc(sm[pre + "nmax"], 1)
                dve.wait_ge(sm[pre + "nmax"], i + 1)
                v.tensor_scalar(nbias[:, q, :], nmax[:, q, :], SM, None, ALU.mult).then_inc(sm[pre + "bias"], 1)

            def sums(pre, q, n, i, count):
                dve.wait_ge(sm[pre + "exp"], count)
                v.tensor_reduce(rsum[:, q, :], esum[:, q, :n], X, ALU.add).then_inc(sm[pre + "rsum"], 1)
                dve.wait_ge(sm[pre + "rsum"], i + 1)
                v.reciprocal(rinv[:, q, :], rsum[:, q, :]).then_inc(sm[pre + "rinv"], 1)

            def residual(pre, i, q):
                dve.wait_ge(sm[pre + "rinv"], i + 1)
                dve.wait_ge(sm[pre + "pv"], i + 1)
                v.scalar_tensor_tensor(u[:, q, :], psO[q][:, :D], rinv[:, q, :], y[:, i, :], ALU.mult,
                                       ALU.add).then_inc(sm[pre + "u"], 1)

            def row_stats(pre, i, q):
                dve.wait_ge(sm[pre + "u"], i + 1)
                v.bn_stats(stat[:, q, :], u[:, q, :]).then_inc(sm[pre + "stat"], 1)

            def row_aggr(pre, i, q):
                dve.wait_ge(sm[pre + "stat"], i + 1)
                if not isinstance(i, int):
                    bridge_dve()
                v.bn_aggr(mv[:, q, :], stat[:, q, :]).then_inc(sm[pre + "agg"], 1)

            def row_var(pre, i, q):
                dve.wait_ge(sm[pre + "agg"], i + 1)
                v.tensor_scalar(veps[:, q, :], mv[:, q, 1:2], EPS, None, ALU.add).then_inc(sm[pre + "var"], 1)

            ROWS = (residual, row_stats, row_aggr, row_var)

            def between(ones_, others):
                for n in range(max(len(ones_), len(others))):
                    for part in (ones_, others):
                        if n < len(part):
                            part[n]()

            def q_lo(t, q, k):
                dve.wait_ge(sm["c_qhi"], t + 1)
                v.tensor_tensor(qT[:, q, 1, :, :], psT[k][:, P:P + D].rearrange("p (k t) -> p k t", k=KD),
                                qT[:, q, 0, :, :], ALU.subtract).then_inc(sm["c_qlo"], 1)

            def c_max(i, q, c):
                maxes("c_", q, c, CW[c], 4 * i + c + 1)

            def c_bias(i, q):
                bias("c_", q, C_CH, i, 4 * i + 4)

            grp = [0]

            def s_los(i, g):
                n = min(4, i + 1 - 4 * g)
                grp[0] += 1
                wait(dve, "s_hi", grp[0])
                k = (grp[0] - 1) % 2
                v.tensor_tensor(probT[:, i % 2, 1, 4 * g:4 * g + n, :],
                                psT[k][:, :n * P].rearrange("p (k t) -> p k t", k=n),
                                probT[:, i % 2, 0, 4 * g:4 * g + n, :], ALU.subtract).then_inc(sm["s_lo"], 1)

            def s_max(i, c):
                maxes("s_", i % 2, c, min(CH, (i + 1) * P - c * CH), S_CH[i] + c + 1)

            def s_bias(i):
                bias("s_", i % 2, chunk_of(i), i, S_CH[i + 1])

            def s_norm(i):
                if i >= 2:
                    wait(dve, "s_y", i - 1)
                normalise("s_", u[:, i % 2, :], i % 2, i)

            s_max(0, 0)
            s_bias(0)
            l0_norm(1)

            def empty_records():
                v.memset(zero.bitcast(U32), 0).then_inc(sm["fill_made"], 1)
                wait(dve, "consts", 19)
                v.memset(fill[:, :, 1], 0).then_inc(sm["fill_made"], 1)
                v.tensor_scalar(fill[:, :, 0], fill[:, :, 0], P - 1, S, ALU.bitwise_and,
                                ALU.bitwise_or).then_inc(sm["fill_made"], 1)

            def later(f, *args):
                return lambda: f(*args)

            for i in range(NT):
                ng = chunk_of(i)
                nch = chunk_of(i + 1) if i + 1 < NT else 0
                for g in range(min(2, ng)):
                    s_los(i, g)
                maxs = [later(s_max, i + 1, c) for c in range(nch)]
                if ng > 2:
                    maxs.insert(2, later(s_los, i, 2))
                if nch:
                    maxs.append(later(s_bias, i + 1))
                if i == NT - 1:
                    maxs = [later(c_max, 0, 0, c) for c in range(C_CH)]
                    maxs.insert(2, later(s_los, i, 2))
                    maxs.append(later(c_bias, 0, 0))
                between(maxs, [later(f, "s_", i - 1, (i - 1) % 2) for f in ROWS] if i else [])
                sums("s_", i % 2, ng, i, S_CH[i + 1])
                if i:
                    s_norm(i - 1)
                if ng > 3:
                    s_los(i, 3)
                if i == 0:
                    empty_records()
                if i in L0_STATS:
                    l0_stats(L0_STATS[i])
                if i in L0_NORM:
                    l0_norm(L0_NORM[i])
                for n in range(sum(SPLITS[:i]), sum(SPLITS[:i + 1])):
                    split_lo(dve, pieces[n], n, n % 2)
                if i - 1 in L0_TRANS:
                    l0_los(L0_TRANS[i - 1])
                if i == NT - 2:
                    q_lo(0, 0, 0)
                    q_lo(1, 1, 1)

            def c_los(i, q, g, nxt2=False):
                n = 4 if g < 3 else 1
                r = P if g < 3 else ZR
                dve.wait_ge(sm["c_hi"], 4 * i + g + 1)
                if nxt2:
                    dve.wait_ge(sm["c_qhi"], i + 3)
                v.tensor_tensor(probT[:r, q, 1, 4 * g:4 * g + n, :],
                                psT[g % 2][:r, :n * P].rearrange("p (k t) -> p k t", k=n),
                                probT[:r, q, 0, 4 * g:4 * g + n, :], ALU.subtract).then_inc(sm["c_lo"], 1)

            def c_norm(i, q):
                if isinstance(i, int) and i < 2:
                    wait(dve, "s_y", NT - 1 + i)
                else:
                    dve.wait_ge(sm["c_y"], i - 1)
                normalise("c_", u[:, q, :], q, i)

            def c_step(i, q, nxt=True, nxt2=True):
                c_los(i, q, 0)
                c_los(i, q, 1)
                before = ("s_", NT - 1) if isinstance(i, int) and i == 0 else ("c_", i - 1)
                maxs = [later(c_max, i + 1, 1 - q, c) for c in range(C_CH)] if nxt else []
                maxs.insert(2, later(c_los, i, q, 2))
                if nxt:
                    maxs.append(later(c_bias, i + 1, 1 - q))
                between(maxs, [later(f, *before, 1 - q) for f in ROWS])
                sums("c_", q, C_CH, i, 4 * i + 4)
                if isinstance(i, int) and i == 0:
                    s_norm(NT - 1)
                else:
                    c_norm(i - 1, 1 - q)
                c_los(i, q, 3, nxt2)
                if nxt2:
                    q_lo(i + 2, q, 1)
                split_cross(split_lo, dve, i)

            for i in range(LOOP[0] + 2):
                c_step(i, i % 2)
            with dve.Fori(LOOP[0] + 2, LOOP[1] - 1, 2) as i:
                c_step(i, 0)
                c_step(i + 1, 1)
            for i in range(LOOP[1], NT - 1):
                c_step(i, i % 2, i + 1 < NT, i + 2 < NT)

            def y_lo(j):
                for k in range(KD):
                    wait(dve, "f_yhi", KD * j + k + 1)
                    v.tensor_tensor(ybT[:, 1, k, :], psY(j)[k][:], ybT[:, 0, k, :], ALU.subtract).then_inc(sm["f_ylo"], 1)

            def hid_lo(j, f):
                wait(dve, "f_hi", KF * j + f + 1)
                v.tensor_tensor(hidT[:, 1, f, :], hid[:, f % 4, :], hidT[:, 0, f, :],
                                ALU.subtract).then_inc(sm["f_lo"], 1)

            def out_tile(j, m):
                n = j * TB + m
                wait(dve, "f_down", n + 1)
                wait(dve, "n_yb", j + 1)
                v.scalar_tensor_tensor(u4[:, m, :], psO[m % 2][:, :D], 1.0 / WS, y[:, n, :], ALU.mult,
                                       ALU.add).then_inc(sm["n_u"], 1)
                wait(dve, "n_u", n + 1)
                v.bn_stats(stat4[:, m, :], u4[:, m, :]).then_inc(sm["n_stat"], 1)

            def out_moments(j):
                wait(dve, "n_stat", TB * (j + 1))
                aggregate4("n_", j)

            def centre(j):
                for m in range(TB):
                    r = v.scalar_tensor_tensor(u4[:, m, :], u4[:, m, :], mv4[:, m, 0:1], vec[:, 0, :],
                                               ALU.subtract, ALU.mult)
                r.then_inc(sm["n_cen"], 1)

            def first_out(j):
                wait(dve, "n_rstd", j + 1)
                wait(dve, "n_cen", j + 1)
                wait(dve, "f_xb", j + 1)
                for m in range(TB):
                    r = v.scalar_tensor_tensor(y[:, j * TB + m, :], u4[:, m, :], rstd4[:, m:m + 1],
                                               xin[:, j % 2, m, :], ALU.mult, ALU.add)
                r.then_inc(sm["n_x1"], 1)

            def x1_stats(j):
                wait(dve, "n_x1", j + 1)
                for m in range(TB):
                    v.bn_stats(stat4[:, m, :], y[:, j * TB + m, :]).then_inc(sm["m_stat"], 1)

            def x1_aggr(j):
                wait(dve, "m_stat", TB * (j + 1))
                aggregate4("m_", j)

            def h_norm(j):
                normalise4("m_", lambda m: y[:, j * TB + m, :], lambda m: h4[:, m, :], j, "m_h")

            def h_lo(j):
                wait(dve, "m_hhi", j + 1)
                v.tensor_tensor(hs[:, :, 1, :], h4, hs[:, :, 0, :], ALU.subtract).then_inc(sm["m_hlo"], 1)

            recf = recs[:].bitcast(F32)

            def choose(j):
                wait(dve, "r_logit", j + 1)
                v.tensor_scalar(lg.rearrange("p m e -> p (m e)"), ps[2][:, :TB * NE], 1.0 / WS, None,
                                ALU.mult).then_inc(sm["r_lg"], 1)
                wait(dve, "r_lg", j + 1)
                for m in range(TB):
                    r = v.max(top[:, m, :], lg[:, m, :])
                link(r)
                for m in range(TB):
                    r = v.max_index(topi[:, m, :], top[:, m, :], lg[:, m, :])
                link(r)
                v.tensor_tensor(dl[:], top[:, :, 1], top[:, :, 0], ALU.subtract).then_inc(sm["r_dl"], 1)
                link(v.tensor_copy(topf[:], topi[:, :, 0:TOP]))
                for c in range(TOP):
                    r = v.tensor_tensor(oh[:, c], iota8[:].unsqueeze(1).broadcast_to([P, TB, NE]),
                                        topf[:, :, c].unsqueeze(2).broadcast_to([P, TB, NE]), ALU.is_equal)
                link(r)
                v.tensor_tensor(cho[:, j * TB:(j + 1) * TB, :], oh[:, 0], oh[:, 1], ALU.add).then_inc(sm["r_cho"], 1)

            def weigh(j):
                b = slice(j * TB, (j + 1) * TB)
                wait(dve, "r_exp", j + 1)
                link(v.tensor_scalar(den[:], ex[:], 1.0, WS, ALU.add, ALU.mult))
                v.reciprocal(recf[:, b, 0, 1], den[:]).then_inc(sm["r_rec"], 1)
                wait(dve, "r_rec", TOP * j + 1)
                v.tensor_tensor(recf[:, b, 1, 1], ex[:], recf[:, b, 0, 1], ALU.mult).then_inc(sm["r_rec"], 1)

            def place(j):
                wait(dve, "r_rank", j + 1)
                v.tensor_tensor(slot, ps[3][:, :TB * NE].rearrange("p (m e) -> p m e", m=TB),
                                ebase[:].unsqueeze(1).broadcast_to([P, TB, NE]), ALU.add).then_inc(sm["r_rk"], 1)
                wait(dve, "r_rk", j + 1)
                for c in range(TOP):
                    link(v.tensor_tensor(prod, slot, oh[:, c], ALU.mult))
                    link(v.tensor_reduce(slotf[:, c, :], prod, X, ALU.add))
                v.tensor_copy(slots[:, :, j * TB:(j + 1) * TB], slotf[:]).then_inc(sm["r_slot"], 1)

            def table_counts(p):
                wait(dve, "r_count", p + 1)
                cut = cuts if p == 2 else cutf
                v.tensor_tensor(used, ps[2][:, CH - NE:].unsqueeze(2).broadcast_to([P, NE, NT]),
                                cut[:].unsqueeze(1).broadcast_to([P, NE, NT]), ALU.is_gt).then_inc(sm["r_used"], 1)
                wait(dve, "r_used", p + 1)

            def table(p):
                _, n0, n1 = PHASES[p]
                nj, n = n1 - n0, NE - 1
                pa, ju, at = past[:, :nj, :], jump[:, :nj, :], slice(n0, n1)
                link(v.tensor_reduce(ntile[:], used, X, ALU.add))
                if p:
                    link(v.tensor_tensor(rem[:], ntile[:], taken[:], ALU.subtract))
                else:
                    link(v.tensor_copy(rem[:], ntile[:]))
                link(v.tensor_tensor(upto, rem[:].unsqueeze(1).broadcast_to([P, NE, NE]), tri8[:], ALU.mult))
                link(v.tensor_reduce(icum[:], upto, X, ALU.add))
                link(v.tensor_tensor(pa, icum[:, :n].unsqueeze(1).broadcast_to([P, nj, n]),
                                     jot[:, :nj].unsqueeze(2).broadcast_to([P, nj, n]), ALU.is_le))
                link(v.tensor_scalar(skip[:], rem[:], -1.0, float(BL), ALU.mult, ALU.add))
                if p:
                    link(v.tensor_tensor(more[:, :n], taken[:, 1:], taken[:, :n], ALU.subtract))
                    link(v.tensor_tensor(skip[:, :n], skip[:, :n], more[:, :n], ALU.add))
                link(v.tensor_tensor(ju, pa, skip[:, :n].unsqueeze(1).broadcast_to([P, nj, n]), ALU.mult))
                v.tensor_reduce(tabf[:, 1, at], ju, X, ALU.add)
                link(v.tensor_reduce(tabf[:, 0, at], pa, X, ALU.add))
                link(v.tensor_scalar(tab[:, 0, at], tabf[:, 0, at], float(NP), None, ALU.mult))
                if p:
                    v.scalar_tensor_tensor(tab[:, 1, at], tabf[:, 1, at], taken[:, 0:1], jot[:, :nj], ALU.add,
                                           ALU.add).then_inc(sm["r_tab"], 1)
                else:
                    v.tensor_tensor(tab[:, 1, at], tabf[:, 1, at], jot[:, :nj], ALU.add).then_inc(sm["r_tab"], 1)
                if p < 2:
                    wait(dve, "r_tab", p + 1)
                    link(v.tensor_tensor(more[:], rem[:], icum[:], ALU.subtract))
                    link(v.tensor_scalar(more[:], more[:], float(nj), 0.0, ALU.add, ALU.max))
                    if p:
                        link(v.tensor_tensor(more[:], more[:], rem[:], ALU.min))
                        link(v.tensor_tensor(taken[:], taken[:], more[:], ALU.add))
                    else:
                        link(v.tensor_tensor(taken[:], more[:], rem[:], ALU.min))

            i, q = NT - 1, (NT - 1) % 2
            c_los(i, q, 0)
            c_los(i, q, 1)
            y_lo(0)
            between([later(c_los, i, q, g) for g in (2, 3)], [later(f, "c_", i - 1, 1 - q) for f in ROWS])
            sums("c_", q, C_CH, i, 4 * i + 4)
            c_norm(i - 1, 1 - q)
            split_cross(split_lo, dve, i)
            for f in range(EARLY):
                hid_lo(0, f)
            for f in ROWS:
                f("c_", i, q)
            c_norm(i, q)
            for j in range(NB):
                for f in range(0 if j else EARLY, KF):
                    hid_lo(j, f)
                    if j:
                        if f == 0:
                            centre(j - 1)
                        if f == 1:
                            first_out(j - 1)
                        if f == 2 and j > 1:
                            weigh(j - 2)
                            place(j - 2)
                            if j == NB - 1:
                                table_counts(0)
                        if f == 3:
                            x1_stats(j - 1)
                        if f == 4:
                            x1_aggr(j - 1)
                if j + 1 < NB:
                    y_lo(j + 1)
                else:
                    table(0)
                split_ff(split_lo, dve, j, (0, 1))
                out_tile(j, 0)
                if j:
                    h_norm(j - 1)
                out_tile(j, 1)
                if j:
                    h_lo(j - 1)
                split_ff(split_lo, dve, j, (2, 3))
                out_tile(j, 2)
                out_tile(j, 3)
                out_moments(j)
                if j:
                    choose(j - 1)
            centre(NB - 1)
            first_out(NB - 1)

            def gated(n, q):
                dve.wait_ge(sm["e_sil"], n + 1)
                v.scalar_tensor_tensor(act[:, q, :], ps[2 * q + 1][:], 1.0 / WS, sil[:, q, :], ALU.mult,
                                       ALU.mult).then_inc(sm["e_act"], 1)

            def act_lo(n, q):
                dve.wait_ge(sm["e_ahi"], n + 1)
                v.tensor_tensor(actT[:, q, 1, :, :].rearrange("p k t -> p (k t)"), psT[q][:],
                                actT[:, q, 0, :, :].rearrange("p k t -> p (k t)"), ALU.subtract).then_inc(sm["e_alo"], 1)

            def weighted(n, q):
                dve.wait_ge(sm["e_down"], n + 1)
                if not (isinstance(n, int) and n < 2):
                    dve.wait_ge(sm["e_add"], 16 * n - 16)
                v.tensor_scalar(ys[:, q, :], psO[q][:, :D], rec.bitcast(F32)[:, n, 1:2], None,
                                ALU.mult).then_inc(sm["e_y"], 1)

            def e_step(n, q):
                gated(n, q)
                act_lo(n - 1, 1 - q)
                weighted(n - 2, q)

            j = NB - 1
            gated(0, 0)
            x1_stats(j)
            gated(1, 1)
            x1_aggr(j)
            act_lo(0, 0)
            for n in range(2, E_LOOP):
                q = n % 2
                gated(n, q)
                if n == LOGITS_AT:
                    choose(j)
                for b, at in ((NB - 2, RANKS2_AT), (NB - 1, RANKS_AT)):
                    if n == at:
                        weigh(b)
                        place(b)
                        table_counts(b - (NB - 3))
                act_lo(n - 1, 1 - q)
                weighted(n - 2, q)
                if n == RANKS2_AT:
                    table(1)
                if n == RANKS2_AT + 1:
                    h_norm(j)
                if n == H_AT - 1:
                    h_lo(j)
                if n == RANKS_AT:
                    table(2)
            with dve.Fori(E_LOOP, NJ - 2, 2) as n:
                e_step(n, 0)
                e_step(n + 1, 1)
            e_step(NJ - 1, 0)
            act_lo(NJ - 1, 0)
            weighted(NJ - 2, 1)
            weighted(NJ - 1, 0)


def kernel(**inputs):
    import concourse.bacc as bacc
    from concourse.bass_utils import run_bass_kernel_spmd

    a = {k: np.asarray(v) for k, v in inputs.items()}
    f = "L0_xattn_"
    ctx_ = a["ctx_1024"][0]
    w13 = np.stack([a["L0_ffn_w1"].transpose(0, 2, 1), a["L0_ffn_w3"].transpose(0, 2, 1)], axis=1)
    w13 = w13.reshape(NE, 2, KD, P, NI).transpose(0, 2, 1, 3, 4).reshape(NE, 2 * KD, P, CH)
    w2t = a["L0_ffn_w2"].transpose(0, 2, 1).reshape(NE, KI // 2, 2, P, D).transpose(0, 1, 3, 2, 4)
    arrays = {
        "x_in": a["x"][0],
        "z_in": ctx_,
        "zT_in": ctx_.T,
        "w1_in": a[f + "w1"],
        "w2_in": a[f + "w2"],
        "wgT_in": a["L0_ffn_wg"].T,
        "we_in": np.concatenate([w13, w2t.reshape(NE, KI // 2, P, CH)], axis=1).reshape(NE * NP, P, CH),
        "b1_in": a[f + "b1"].reshape(KF, P).T,
        "rows_in": np.concatenate([a[f + n] for n in ("g1", "beta1", "g2", "beta2", "b2", "g3", "beta3")]),
    }
    arrays = {k: np.ascontiguousarray(v) for k, v in arrays.items()}
    nc = bacc.Bacc("TRN2", target_bir_lowering=False, num_devices=1)
    args = [nc.dram_tensor(k, v.shape, mybir.dt.from_np(v.dtype), kind="ExternalInput").ap()
            for k, v in arrays.items()]
    out = nc.dram_tensor("out", (S + P, D), F32, kind="ExternalOutput").ap()
    xattn_ffn_moe(nc, *args, out)
    r = run_bass_kernel_spmd(nc, [arrays], core_ids=[0])
    return r.results[0]["out"][:S].reshape(1, S, D)
```
